# Optimizing a Trainium2 kernel written in Bass

```python
import numpy as np
import jax
import jax.numpy as jnp

def _softmax(x, axis=-1):
    return jax.nn.softmax(x, axis=axis)

def _gelu(x):
    return jax.nn.gelu(x, approximate=True)

def _silu(x):
    return jax.nn.silu(x)

def _sigmoid(x):
    return jax.nn.sigmoid(x)

def _layernorm(x, axis=-1, eps=1e-05):
    m = jnp.mean(x, axis=axis, keepdims=True)
    v = jnp.var(x, axis=axis, keepdims=True)
    return (x - m) / jnp.sqrt(v + eps)

def _scatter_add(tgt, idx, src, axis=0):
    return tgt.at[idx].add(src)

def _segment_sum(src, seg, n):
    return jax.ops.segment_sum(src, seg, n)
kernel_name = 'mk_gnn_ffn_d2_gnn_r8_ec4ae7'

def setup_inputs(seed: int=0):
    np.random.seed(seed)
    _w = jnp.asarray

    def _rec_inputs():
        import jax
        import jax.numpy as jnp
        _gk = jax.random.key(seed)
        x = -0.0003713 + 1 * jax.random.normal(jax.random.fold_in(_gk, 1), (3125, 512), jnp.float32)
        _s = jax.random.randint(jax.random.fold_in(_gk, 2), (25000,), 0, 3125, jnp.int32)
        _d = jax.random.randint(jax.random.fold_in(_gk, 3), (25000,), 0, 3125, jnp.int32)
        _loop = jnp.arange(3125, dtype=jnp.int32)
        src = jnp.concatenate([_s, _d, _loop])
        dst = jnp.concatenate([_d, _s, _loop])
        _o = jnp.argsort(dst, stable=True)
        src = src[_o]
        dst = dst[_o]
        return (x, src, dst)
    x, src, dst = _rec_inputs()

    def _L0_gnn_setup():
        import jax, jax.numpy as jnp
        import numpy as np
        N = 3125
        M = 18750
        D = 512
        H = 8
        DK = 64
        DV = 64
        key = jax.random.key(seed)
        ks = jax.random.split(key, 8)
        x = jax.random.normal(ks[0], (N, D), jnp.float32)
        edge_index = jax.random.randint(ks[1], (2, M), 0, N).astype(jnp.int32)
        s_in = 1.0 / np.sqrt(D).astype(np.float32)
        s_ff = 1.0 / np.sqrt(H * DV).astype(np.float32)
        Wk = jax.random.normal(ks[2], (D, H * DK), jnp.float32) * s_in
        Wq = jax.random.normal(ks[3], (D, H * DK), jnp.float32) * s_in
        Wv = jax.random.normal(ks[4], (D, H * DV), jnp.float32) * s_in
        Wff = jax.random.normal(ks[5], (H * DV, D), jnp.float32) * s_ff
        bk = jnp.zeros((H * DK,), jnp.float32)
        bq = jnp.zeros((H * DK,), jnp.float32)
        bv = jnp.zeros((H * DV,), jnp.float32)
        bff = jnp.zeros((D,), jnp.float32)
        return {'x': x, 'edge_index': edge_index, 'Wk': Wk, 'bk': bk, 'Wq': Wq, 'bq': bq, 'Wv': Wv, 'bv': bv, 'Wff': Wff, 'bff': bff}
    _L0_gnn_all = _L0_gnn_setup()
    _L0_gnn_in = {k: v for k, v in _L0_gnn_all.items() if k in ('Wk', 'bk', 'Wq', 'bq', 'Wv', 'bv', 'Wff', 'bff')}
    del _L0_gnn_all

    def _L0_ffn_setup():
        import jax, jax.numpy as jnp
        import numpy as np
        MARK_AX, OP_ADD, OP_SUB = (0, 1, 2)
        ALU_LO, ALU_HI = (16, 32)
        AX_CARRY_LO, AX_CARRY_HI = (48, 64)
        OPCODE_BASE = 80
        OUTPUT_LO, OUTPUT_HI, CARRY = (128, 144, 160)
        NIB_A, NIB_B, OP_START = (0, 1, 10)
        RESULT, CARRY_OUT = (100, 101)
        GE_POS, GE_DIM = (8, 160)
        OPC_ADD, OPC_SUB = (25, 26)
        B, S, D = (8, 512, 512)

        def _decode_nibble(x, base):
            return jnp.argmax(x[..., base:base + 16] > 0.5, axis=-1).astype(x.dtype)

        def _pipeline(h, W, b):
            for i in range(3):
                h = jnp.einsum('bspd,od->bspo', h, W[i]) + b[i]
                if i < 2:
                    h = jax.nn.relu(h)
            return h
        key = jax.random.key(seed)
        kx, k1, k2, k3, k4 = jax.random.split(key, 5)
        x_bd = jax.random.uniform(kx, (B, S, D), dtype=jnp.float32)
        Wa = jax.random.normal(k1, (3, GE_DIM, GE_DIM), dtype=jnp.float32) * 0.05
        ba = jax.random.normal(k2, (3, GE_DIM), dtype=jnp.float32) * 0.05
        Ws = jax.random.normal(k3, (3, GE_DIM, GE_DIM), dtype=jnp.float32) * 0.05
        bs = jax.random.normal(k4, (3, GE_DIM), dtype=jnp.float32) * 0.05
        return {'x_bd': x_bd, 'Wa': Wa, 'ba': ba, 'Ws': Ws, 'bs': bs}
    _L0_ffn_all = _L0_ffn_setup()
    _L0_ffn_in = {k: v for k, v in _L0_ffn_all.items() if k in ('Wa', 'ba', 'Ws', 'bs')}
    del _L0_ffn_all

    def _L1_gnn_setup():
        import jax, jax.numpy as jnp
        import numpy as np
        N = 1250
        E = 20000
        IN = 512
        HID = 512
        OUT = 512

        def _gcn_norm(edge_index, n):
            loops = jnp.arange(n, dtype=edge_index.dtype)
            row = jnp.concatenate([edge_index[0], loops])
            col = jnp.concatenate([edge_index[1], loops])
            deg = jax.ops.segment_sum(jnp.ones_like(col, jnp.float32), col, num_segments=n)
            dis = jnp.where(deg > 0, jax.lax.rsqrt(jnp.maximum(deg, 1.0)), 0.0)
            norm = dis[row] * dis[col]
            return (row, col, norm)

        def _gcn_layer(x, row, col, norm, W, b, n):
            h = x @ W
            msg = h[row] * norm[:, None]
            out = jax.ops.segment_sum(msg, col, num_segments=n)
            return out + b
        key = jax.random.key(seed)
        ks = jax.random.split(key, 8)
        x = jax.random.normal(ks[0], (N, IN), dtype=jnp.float32)
        edge_index = jax.random.randint(ks[1], (2, E), 0, N, dtype=jnp.int64)

        def w(k, fi, fo):
            return jax.random.normal(k, (fi, fo), dtype=jnp.float32) * (1.0 / np.sqrt(fi)).astype(np.float32)
        return {'x': x, 'edge_index': edge_index, 'W1': w(ks[2], IN, HID), 'b1': jnp.zeros((HID,), jnp.float32), 'W2': w(ks[3], HID, HID), 'b2': jnp.zeros((HID,), jnp.float32), 'W3': w(ks[4], HID, OUT), 'b3': jnp.zeros((OUT,), jnp.float32)}
    _L1_gnn_all = _L1_gnn_setup()
    _L1_gnn_in = {k: v for k, v in _L1_gnn_all.items() if k in ('W1', 'b1', 'W2', 'b2', 'W3', 'b3')}
    del _L1_gnn_all

    def _L1_ffn_setup():
        import jax, jax.numpy as jnp
        import numpy as np
        DIM = 512
        FFN_DIM = 1408
        GROUP = 128
        EPS = 1e-05

        def _quantize_weight(w, group_size):
            o, i = w.shape
            wg = w.reshape(o, i // group_size, group_size)
            scale = jnp.mean(jnp.abs(wg), axis=-1, keepdims=True) + EPS
            wq = jnp.clip(jnp.round(wg / scale), -1.0, 1.0) * scale
            return wq.reshape(o, i)

        def _bitlinear(x, w, group_size=GROUP):
            wq = w + jax.lax.stop_gradient(_quantize_weight(w, group_size) - w)
            return jnp.einsum('bsd,fd->bsf', x, wq)
        key = jax.random.key(seed)
        k_x, k_g, k_u, k_d = jax.random.split(key, 4)
        x = jax.random.normal(k_x, (8, 512, DIM), dtype=jnp.float32)
        sd_in = 1.0 / np.sqrt(DIM)
        sd_ffn = 1.0 / np.sqrt(FFN_DIM)
        w_gate = jax.random.normal(k_g, (FFN_DIM, DIM), dtype=jnp.float32) * sd_in
        w_up = jax.random.normal(k_u, (FFN_DIM, DIM), dtype=jnp.float32) * sd_in
        w_down = jax.random.normal(k_d, (DIM, FFN_DIM), dtype=jnp.float32) * sd_ffn
        return {'x': x, 'w_gate': w_gate, 'w_up': w_up, 'w_down': w_down}
    _L1_ffn_all = _L1_ffn_setup()
    _L1_ffn_in = {k: v for k, v in _L1_ffn_all.items() if k in ('w_gate', 'w_up', 'w_down')}
    del _L1_ffn_all
    return {'x': x, 'src': src, 'dst': dst, 'L0_gnn_Wk': _L0_gnn_in['Wk'], 'L0_gnn_bk': _L0_gnn_in['bk'], 'L0_gnn_Wq': _L0_gnn_in['Wq'], 'L0_gnn_bq': _L0_gnn_in['bq'], 'L0_gnn_Wv': _L0_gnn_in['Wv'], 'L0_gnn_bv': _L0_gnn_in['bv'], 'L0_gnn_Wff': _L0_gnn_in['Wff'], 'L0_gnn_bff': _L0_gnn_in['bff'], 'L0_ffn_Wa': _L0_ffn_in['Wa'], 'L0_ffn_ba': _L0_ffn_in['ba'], 'L0_ffn_Ws': _L0_ffn_in['Ws'], 'L0_ffn_bs': _L0_ffn_in['bs'], 'L1_gnn_W1': _L1_gnn_in['W1'], 'L1_gnn_b1': _L1_gnn_in['b1'], 'L1_gnn_W2': _L1_gnn_in['W2'], 'L1_gnn_b2': _L1_gnn_in['b2'], 'L1_gnn_W3': _L1_gnn_in['W3'], 'L1_gnn_b3': _L1_gnn_in['b3'], 'L1_ffn_w_gate': _L1_ffn_in['w_gate'], 'L1_ffn_w_up': _L1_ffn_in['w_up'], 'L1_ffn_w_down': _L1_ffn_in['w_down']}

def reference(x, src, dst, L0_gnn_Wk, L0_gnn_bk, L0_gnn_Wq, L0_gnn_bq, L0_gnn_Wv, L0_gnn_bv, L0_gnn_Wff, L0_gnn_bff, L0_ffn_Wa, L0_ffn_ba, L0_ffn_Ws, L0_ffn_bs, L1_gnn_W1, L1_gnn_b1, L1_gnn_W2, L1_gnn_b2, L1_gnn_W3, L1_gnn_b3, L1_ffn_w_gate, L1_ffn_w_up, L1_ffn_w_down):
    import jax
    import jax.numpy as jnp

    def _L0_gnn_ref(x, edge_index, Wk, bk, Wq, bq, Wv, bv, Wff, bff):
        import jax, jax.numpy as jnp
        import numpy as np
        N = 3125
        M = 18750
        D = 512
        H = 8
        DK = 64
        DV = 64
        K = (x @ Wk + bk).reshape(-1, H, DK)
        Q = (x @ Wq + bq).reshape(-1, H, DK)
        V = (x @ Wv + bv).reshape(-1, H, DV)
        senders, receivers = (edge_index[0], edge_index[1])
        att = jnp.einsum('mhd,mhd->mh', Q[receivers], K[senders]) / np.sqrt(DK).astype(np.float32)
        att = jnp.exp(att + 3.0 - att.max())
        ssum = jax.ops.segment_sum(att, receivers, num_segments=N)
        denom = ssum[receivers]
        att = jnp.where(denom == 0, 0.0, att / jnp.where(denom == 0, 1.0, denom))
        msg = att[..., None] * V[senders]
        agg = jax.ops.segment_sum(msg, receivers, num_segments=N)
        return agg.reshape(-1, H * DV) @ Wff + bff

    def _L0_ffn_ref(x_bd, Wa, ba, Ws, bs):
        import jax, jax.numpy as jnp
        import numpy as np
        MARK_AX, OP_ADD, OP_SUB = (0, 1, 2)
        ALU_LO, ALU_HI = (16, 32)
        AX_CARRY_LO, AX_CARRY_HI = (48, 64)
        OPCODE_BASE = 80
        OUTPUT_LO, OUTPUT_HI, CARRY = (128, 144, 160)
        NIB_A, NIB_B, OP_START = (0, 1, 10)
        RESULT, CARRY_OUT = (100, 101)
        GE_POS, GE_DIM = (8, 160)
        OPC_ADD, OPC_SUB = (25, 26)
        B, S, D = (8, 512, 512)

        def _decode_nibble(x, base):
            return jnp.argmax(x[..., base:base + 16] > 0.5, axis=-1).astype(x.dtype)

        def _pipeline(h, W, b):
            for i in range(3):
                h = jnp.einsum('bspd,od->bspo', h, W[i]) + b[i]
                if i < 2:
                    h = jax.nn.relu(h)
            return h
        x = x_bd
        Bsz, seq, _ = x.shape
        x_ge = jnp.zeros((Bsz, seq, GE_POS, GE_DIM), dtype=x.dtype)
        x_ge = x_ge.at[..., 0, NIB_A].set(_decode_nibble(x, ALU_LO))
        x_ge = x_ge.at[..., 1, NIB_A].set(_decode_nibble(x, ALU_HI))
        x_ge = x_ge.at[..., 0, NIB_B].set(_decode_nibble(x, AX_CARRY_LO))
        x_ge = x_ge.at[..., 1, NIB_B].set(_decode_nibble(x, AX_CARRY_HI))
        x_ge = x_ge.at[..., :, OP_START + OPC_ADD].set(x[..., OPCODE_BASE + OPC_ADD][..., None])
        x_ge = x_ge.at[..., :, OP_START + OPC_SUB].set(x[..., OPCODE_BASE + OPC_SUB][..., None])
        mark = x[..., MARK_AX] > 0.5
        m_add = mark & (x[..., OP_ADD] > 0.5)
        m_sub = mark & ~(x[..., OP_ADD] > 0.5) & (x[..., OP_SUB] > 0.5)
        active = (m_add | m_sub).astype(x.dtype)
        y_add = _pipeline(x_ge, Wa, ba)
        y_sub = _pipeline(x_ge, Ws, bs)
        y = jnp.where(m_add[..., None, None], y_add, jnp.where(m_sub[..., None, None], y_sub, x_ge))
        res_lo = jnp.clip(jnp.round(y[..., 0, RESULT]), 0, 15).astype(jnp.int32)
        res_hi = jnp.clip(jnp.round(y[..., 1, RESULT]), 0, 15).astype(jnp.int32)
        oh_lo = jax.nn.one_hot(res_lo, 16, dtype=x.dtype) * active[..., None]
        oh_hi = jax.nn.one_hot(res_hi, 16, dtype=x.dtype) * active[..., None]
        carry = (jnp.round(y[..., 1, CARRY_OUT]) > 0.5).astype(x.dtype) * active
        out = x
        out = out.at[..., OUTPUT_LO:OUTPUT_LO + 16].add(2.0 * oh_lo)
        out = out.at[..., OUTPUT_HI:OUTPUT_HI + 16].add(2.0 * oh_hi)
        out = out.at[..., CARRY].add(carry)
        return out

    def _L1_gnn_ref(x, edge_index, W1, b1, W2, b2, W3, b3):
        import jax, jax.numpy as jnp
        import numpy as np
        N = 1250
        E = 20000
        IN = 512
        HID = 512
        OUT = 512

        def _gcn_norm(edge_index, n):
            loops = jnp.arange(n, dtype=edge_index.dtype)
            row = jnp.concatenate([edge_index[0], loops])
            col = jnp.concatenate([edge_index[1], loops])
            deg = jax.ops.segment_sum(jnp.ones_like(col, jnp.float32), col, num_segments=n)
            dis = jnp.where(deg > 0, jax.lax.rsqrt(jnp.maximum(deg, 1.0)), 0.0)
            norm = dis[row] * dis[col]
            return (row, col, norm)

        def _gcn_layer(x, row, col, norm, W, b, n):
            h = x @ W
            msg = h[row] * norm[:, None]
            out = jax.ops.segment_sum(msg, col, num_segments=n)
            return out + b
        n = x.shape[0]
        row, col, norm = _gcn_norm(edge_index, n)
        h = _gcn_layer(x, row, col, norm, W1, b1, n)
        h = jax.nn.relu(h)
        h = _gcn_layer(h, row, col, norm, W2, b2, n)
        h = jax.nn.relu(h)
        h = _gcn_layer(h, row, col, norm, W3, b3, n)
        return h

    def _L1_ffn_ref(x, w_gate, w_up, w_down):
        import jax, jax.numpy as jnp
        import numpy as np
        DIM = 512
        FFN_DIM = 1408
        GROUP = 128
        EPS = 1e-05

        def _quantize_weight(w, group_size):
            o, i = w.shape
            wg = w.reshape(o, i // group_size, group_size)
            scale = jnp.mean(jnp.abs(wg), axis=-1, keepdims=True) + EPS
            wq = jnp.clip(jnp.round(wg / scale), -1.0, 1.0) * scale
            return wq.reshape(o, i)

        def _bitlinear(x, w, group_size=GROUP):
            wq = w + jax.lax.stop_gradient(_quantize_weight(w, group_size) - w)
            return jnp.einsum('bsd,fd->bsf', x, wq)
        gate = _bitlinear(x, w_gate)
        up = _bitlinear(x, w_up)
        h = jax.nn.silu(gate) * up
        return _bitlinear(h, w_down)
    edge_index = jnp.stack([src, dst])
    x = x + _L0_gnn_ref(_layernorm(x, axis=-1), edge_index, L0_gnn_Wk, L0_gnn_bk, L0_gnn_Wq, L0_gnn_bq, L0_gnn_Wv, L0_gnn_bv, L0_gnn_Wff, L0_gnn_bff)
    x = x + _L0_ffn_ref(_layernorm(x, axis=-1)[None], L0_ffn_Wa, L0_ffn_ba, L0_ffn_Ws, L0_ffn_bs)[0]
    x = x + _L1_gnn_ref(_layernorm(x, axis=-1), edge_index, L1_gnn_W1, L1_gnn_b1, L1_gnn_W2, L1_gnn_b2, L1_gnn_W3, L1_gnn_b3)
    x = x + _L1_ffn_ref(_layernorm(x, axis=-1)[None], L1_ffn_w_gate, L1_ffn_w_up, L1_ffn_w_down)[0]
    return x

_drawn_inputs = setup_inputs


def setup_inputs(seed=0):
    import zlib

    import numpy as np

    out = dict(_drawn_inputs(seed))
    spreads = {'L0_gnn_bk': (0.0, 0.8),
     'L0_gnn_bq': (0.0, 0.276),
     'L0_gnn_bv': (0.0, 0.1),
     'L0_gnn_bff': (0.0, 0.1),
     'L1_gnn_b1': (0.0, 0.478),
     'L1_gnn_b2': (0.0, 0.1),
     'L1_gnn_b3': (0.0, 0.1)}
    factors = {}
    for name, (base, spread) in spreads.items():
        noise = np.random.default_rng([zlib.crc32(name.encode()), seed]).standard_normal(out[name].shape)
        drawn = base * np.exp(spread * noise) if base else spread * noise
        out[name] = jnp.asarray(drawn.astype(out[name].dtype))
    for name, factor in factors.items():
        out[name] = (out[name] * factor).astype(out[name].dtype)
    return out
```

```python
from contextlib import ExitStack, contextmanager

import numpy as np

import concourse.bass as bass
from concourse import mybir

F32 = mybir.dt.float32
I32 = mybir.dt.int32
U32 = mybir.dt.uint32
F32R = mybir.dt.float32r
ALU = mybir.AluOpType
ACT = mybir.ActivationFunctionType
AX = mybir.AxisListType

P = 128
N, D = 3125, 512
T = 125
NT = N // T
KT = D // P
H, DH = 8, 64
E = 53125
EC = E // T
STEP = 256
U = 8
RING = 4
NS = -(-((E + NT * (STEP - 1)) // STEP) // U) * U
SC = NS * STEP // P
AHEAD = 2 * RING
SCAT = 25
AW = D + H + 1
GE = 160
FF = 1408
FT = FF // P
EPS = 1e-5
RNE = 12582912.0


def rows(i):
    return bass.ds(i * T, T)


def over(eng, count, *stages, peel=0):
    most = max(lag for lag, _ in stages)
    first = most + most % 2
    last = first + (count - peel - first) // 2 * 2

    def items(n, parity):
        for lag, f in stages:
            if not isinstance(n, int) or 0 <= n - lag < count:
                f(n - lag, (parity - lag) % 2)

    for n in range(first):
        items(n, n % 2)
    with eng.Fori(first, last - 1, 2) as n:
        items(n, 0)
        items(n + 1, 1)
    for n in range(last, count + most):
        items(n, n % 2)


def lap(i, s):
    return 8 * i + (16 - 8 * s)


@contextmanager
def phase(nc, dmas=(), reached=0):
    with ExitStack() as stack:
        used = []

        def sem(name):
            used.append(stack.enter_context(nc.semaphore(name)))
            return used[-1]

        yield sem
        with nc.Block() as block:
            @block.sync
            def _(sp):
                for s in used:
                    sp.sem_clear(s)

            if dmas:
                @block.gpsimd
                def _(pool):
                    for s in dmas:
                        pool.wait_ge(s, reached)
                    pool.dma_reset()
                    for s in dmas:
                        pool.sem_clear(s)


class Chain:

    def __init__(self, eng, sem, per=0):
        self.eng, self.sem, self.per, self.base, self.n = eng, sem, per, 0, 0

    def start(self, i):
        self.base, self.n = i * self.per, 0

    def link(self, ins):
        self.n += 1
        ins.then_inc(self.sem, 1)
        self.eng.wait_ge(self.sem, self.base + self.n)

    def end(self):
        assert self.n == self.per, (self.n, self.per)


def build(nc, x, src, dst, Wk, bk, Wq, bq, Wv, bv, Wff, bff, Wa, ba, Ws, bs,
          W1, b1, W2, b2, W3, b3, w_gate, w_up, w_down, out, stop_after=99):
    dram = lambda name, shape, dt=F32: nc.dram_tensor(name, shape, dt, kind="Internal").ap()
    slots_d = dram("slots_d", [P * SC, 2], I32)
    k_d, v_d = dram("k_d", [N, D]), dram("v_d", [N, D])
    g_d = [dram("g0_d", [N, D]), dram("g1_d", [N, D])]
    wT_d = [dram("wgT_d", [P, KT, FF]), dram("wuT_d", [P, KT, FF]), dram("wdT_d", [P, FT, D])]

    with ExitStack() as whole:
        def sb_in(stack):
            return lambda name, shape, dt=F32: stack.enter_context(nc.sbuf_tensor(name, shape, dt))

        sb = sb_in(whole)

        landed = [whole.enter_context(nc.semaphore(f"landed{r}")) for r in range(RING)]
        ident = sb("ident", [P, P])
        eps = sb("eps", [P, 1])
        graph = ExitStack()
        gb = sb_in(graph)
        iota_t = gb("iota_t", [P, T])
        slot_src = gb("slot_src", [P, SC + AHEAD], U32)
        slot_dst = gb("slot_dst", [P, SC + AHEAD])
        step_tile = gb("step_tile", [1, NS], I32)
        e9 = gb("e9", [P, SC * (H + 1)])
        dis = gb("dis", [P, NT])
        acc = gb("acc", [P, NT * AW])
        nibble_w = nibble_weights(gb)

        deal = ExitStack()
        addr = sb_in(deal)("addr", [P, EC], U32)
        pair = sb_in(deal)("pair", [P, EC, 2], I32)
        place_edges(nc, sb_in, dict(ident=ident, eps=eps, iota_t=iota_t, slot_src=slot_src, slot_dst=slot_dst,
                                    step_tile=step_tile, e9=e9, x_sb=acc, addr=addr, pair=pair), x, src, dst, slots_d,
                    nibble_w, Wa, ba, Ws, bs)
        if stop_after == 0:
            return
        project(nc, sb_in, ident, eps, acc, Wq, bq, Wk, bk, Wv, bv, k_d, v_d,
                addr, pair, slots_d, slot_src, slot_dst, w_gate, w_up, w_down, wT_d,
                landed[0])
        deal.close()
        if stop_after == 1:
            return
        score_pass(nc, sb_in, ident, iota_t, slot_src, slot_dst, step_tile, e9, acc, k_d, landed)
        if stop_after == 2:
            return
        softmax_weights(nc, sb_in, slot_dst, e9, acc)
        aggregate(nc, sb_in, "att", iota_t, slot_src, slot_dst, step_tile, v_d, acc, e9, landed)
        if stop_after == 3:
            return
        gcn = ExitStack()
        x2 = sb_in(gcn)("x2", [P, NT * D])
        after_attention(nc, sb_in, ident, eps, x, Wff, bff, nibble_w, acc, dis, x2, g_d[0])
        if stop_after == 4:
            return
        for n, (W, b) in enumerate(((W1, b1), (W2, b2), (W3, b3))):
            aggregate(nc, sb_in, f"gcn{n}", iota_t, slot_src, slot_dst, step_tile, g_d[n % 2], acc, None,
                      landed)
            gcn_dense(nc, sb_in, n, ident, W, b, acc, dis, x2, g_d[(n + 1) % 2])
        gcn.close()
        graph.close()
        swiglu(nc, sb_in, ident, eps, wT_d, g_d[1], out)


def place_edges(nc, sb_in, c, x, src, dst, slots_d, nibble_w, Wa, ba, Ws, bs):
    ident, iota_t, slot_dst, step_tile, e9 = c["ident"], c["iota_t"], c["slot_dst"], c["step_tile"], c["e9"]
    x_sb, addr, pay = c["x_sb"], c["addr"], c["pair"]
    with phase(nc) as sem, ExitStack() as ph:
        sb = sb_in(ph)
        iota_i = sb("iota_i", [P, T], I32)
        tri = sb("tri", [P, P])
        ones = sb("ones", [P, P])
        slot0_i = sb("slot0_i", [1, NS], I32)
        slot0 = sb("slot0", [1, NS])
        tile_f = sb("tile_f", [1, NS])
        blank = sb("blank", [P, SC, 2], I32)
        edges = sb("edges", [P, 2, EC], I32)
        dst_f = sb("dst_f", [P, EC])
        tile_of = sb("tile_of", [P, EC])
        local = sb("local", [P, EC])
        member = sb("member", [P, NT * EC])
        prefix = sb("prefix", [P, NT * EC])
        cnt = sb("cnt", [P, NT])
        base = sb("base", [P, NT])
        size_i = sb("size_i", [P, NT], I32)
        size = sb("size", [P, NT])
        end = sb("end", [P, NT])
        adj = sb("adj", [P, NT])
        pos = sb("pos", [P, EC])
        pos_i = sb("pos_i", [P, EC], I32)
        part_i = sb("part_i", [P, EC], I32)
        part = sb("part", [P, EC])
        pcount = ph.enter_context(nc.psum_tensor("pcount", [P, 2, 512], F32))
        pw = ph.enter_context(nc.psum_tensor("pw", [P, 2, 2, 512], F32))
        nibble_in, w2_turned = sem("nibble_in"), sem("w2_turned")
        nibble_loads = 16 * 2 * (5 + 6 + 1)

        edges_in, pool_consts, blank_ready = sem("edges_in"), sem("pool_consts"), sem("blank_ready")
        blank_out, chain, cnt_ready, counted = sem("blank_out"), sem("deal_chain"), sem("cnt_ready"), sem("counted")
        tri0, id0, x_loaded = sem("tri0"), sem("id0"), sem("x_loaded")
        block = ph.enter_context(nc.Block())

        @block.sync
        def _(sp):
            sp.dma_start(edges[0:T, 0, :], src.rearrange("(p c) -> p c", p=T)).then_inc(edges_in, 16)
            sp.dma_start(edges[0:T, 1, :], dst.rearrange("(p c) -> p c", p=T)).then_inc(edges_in, 16)
            for t in range(0, NT, 5):
                sp.dma_start(x_sb[0:T, t * D:(t + 5) * D].rearrange("p (t d) -> p t d", d=D),
                             x[t * T:(t + 5) * T, :].rearrange("(t p) d -> p t d", p=T)).then_inc(x_loaded, 16)
            load_nibble_weights(nc, sp, nibble_w, nibble_in, Wa, ba, Ws, bs)
            sp.wait_ge(blank_ready, 2)
            sp.dma_start(slots_d.rearrange("(p c) two -> p c two", p=P), blank[:]).then_inc(blank_out, 16)
            sp.wait_ge(blank_out, 16)
            sp.wait_ge(x_loaded, 16 * (NT // 5))

        @block.gpsimd
        def _(pool):
            nc.gpsimd.iota(iota_i[:], [[1, T]], base=0, channel_multiplier=0).then_inc(pool_consts, 1)
            nc.gpsimd.iota(slot0_i[:], [[STEP, NS]], base=0, channel_multiplier=0).then_inc(pool_consts, 1)
            nc.gpsimd.memset(tri[:], 1.0).then_inc(tri0, 1)
            nc.gpsimd.memset(ident[:], 0.0).then_inc(id0, 1)
            pool.wait_ge(tri0, 1)
            nc.gpsimd.affine_select(out=tri[:], in_=tri[:], compare_op=ALU.is_gt, fill=0.0, base=0,
                                    pattern=[[1, P]], channel_multiplier=-1).then_inc(pool_consts, 1)
            pool.wait_ge(id0, 1)
            nc.gpsimd.affine_select(out=ident[:], in_=ident[:], compare_op=ALU.not_equal, fill=1.0, base=0,
                                    pattern=[[1, P]], channel_multiplier=-1).then_inc(pool_consts, 1)

        @block.tensor
        def _(pe):
            pe.wait_ge(pool_consts, 4)
            pe.wait_ge(nibble_in, nibble_loads)
            for q in range(2):
                for n, o, m in GE_PARTS:
                    for n2, o2, m2 in GE_PARTS:
                        t = nc.tensor.transpose(pw[0:m, q, n, o2:o2 + m2], nibble_w["w2n"][0:m2, q, n2, o:o + m],
                                                ident[0:m2, 0:m2])
            t.then_inc(w2_turned, 1)
            pe.wait_ge(cnt_ready, 2)
            nc.tensor.matmul(pcount[0:T, 0, 0:NT], tri[0:T, 0:T], cnt[0:T, :], start=True, stop=True)
            nc.tensor.matmul(pcount[0:T, 1, 0:NT], ones[0:T, 0:T], cnt[0:T, :],
                             start=True, stop=True).then_inc(counted, 1)

        @block.vector
        def _(dve):
            done = [0]

            def link(ins):
                done[0] += 1
                ins.then_inc(chain, 1)
                dve.wait_ge(chain, done[0])

            nc.vector.memset(blank[:, :, 0:1], 0).then_inc(blank_ready, 1)
            nc.vector.memset(blank[:, :, 1:2], -1).then_inc(blank_ready, 1)
            nc.vector.memset(ones[:], 1.0).then_inc(cnt_ready, 1)
            nc.vector.memset(c["eps"][:], EPS)
            nc.vector.memset(e9[:], 1.0)
            nc.vector.memset(slot_dst[:, SC:SC + AHEAD], -1.0)
            nc.vector.memset(c["slot_src"][:, SC:SC + AHEAD], 0)
            dve.wait_ge(edges_in, 32)
            nc.vector.tensor_copy(pay[0:T, :, 0:1], edges[0:T, 0, :].rearrange("p (c o) -> p c o", o=1))
            link(nc.vector.tensor_copy(dst_f[0:T, :], edges[0:T, 1, :]))
            link(nc.vector.tensor_scalar(tile_of[0:T, :], dst_f[0:T, :], float(T), None, ALU.is_ge))
            for t in range(2, NT):
                link(nc.vector.scalar_tensor_tensor(out=tile_of[0:T, :], in0=dst_f[0:T, :], scalar=float(t * T),
                                                    in1=tile_of[0:T, :], op0=ALU.is_ge, op1=ALU.add))
            link(nc.vector.scalar_tensor_tensor(out=local[0:T, :], in0=tile_of[0:T, :], scalar=-float(T),
                                                in1=dst_f[0:T, :], op0=ALU.mult, op1=ALU.add))
            nc.vector.tensor_copy(pay[0:T, :, 1:2], local[0:T, :].rearrange("p (c o) -> p c o", o=1))
            for t in range(NT):
                m = nc.vector.tensor_scalar(member[0:T, t * EC:(t + 1) * EC], tile_of[0:T, :], float(t), None,
                                            ALU.is_equal)
            link(m)
            link(nc.vector.tensor_tensor_scan(prefix[0:T, :], ones[0:T, 0:1].to_broadcast([T, NT * EC]),
                                              member[0:T, :], 0.0, ALU.mult, ALU.add))
            pre = prefix[0:T, :].rearrange("p (t c) -> p t c", t=NT)
            nc.vector.memset(base[0:T, 0:1], 0.0)
            link(nc.vector.tensor_copy(base[0:T, 1:NT], pre[:, 0:NT - 1, EC - 1]))
            nc.vector.tensor_tensor(cnt[0:T, :], pre[:, :, EC - 1], base[0:T, :],
                                    ALU.subtract).then_inc(cnt_ready, 1)
            dve.wait_ge(w2_turned, 1)
            for q in range(2):
                for n, o, m in GE_PARTS:
                    nc.vector.tensor_copy(nibble_w["w2"][0:m, q, n, :], pw[0:m, q, n, 0:GE])
            dve.wait_ge(counted, 1)
            link(nc.vector.tensor_scalar(size_i[0:T, :], pcount[0:T, 1, 0:NT], float(STEP - 1), None, ALU.add))
            link(nc.vector.tensor_scalar(size_i[0:T, :], size_i[0:T, :], -STEP, None, ALU.bitwise_and))
            link(nc.vector.tensor_copy(size[0:T, :], size_i[0:T, :]))
            link(nc.vector.tensor_tensor_scan(end[0:T, :], ones[0:T, 0:NT], size[0:T, :], 0.0, ALU.mult, ALU.add))
            link(nc.vector.tensor_tensor(adj[0:T, :], end[0:T, :], size[0:T, :], ALU.subtract))
            link(nc.vector.tensor_tensor(adj[0:T, :], adj[0:T, :], base[0:T, :], ALU.subtract))
            link(nc.vector.scalar_tensor_tensor(out=adj[0:T, :], in0=pcount[0:T, 0, 0:NT], scalar=-1.0,
                                                in1=adj[0:T, :], op0=ALU.add, op1=ALU.add))
            for t in range(NT):
                s = slice(t * EC, (t + 1) * EC)
                m = nc.vector.scalar_tensor_tensor(out=prefix[0:T, s], in0=prefix[0:T, s], scalar=adj[0:T, t:t + 1],
                                                   in1=member[0:T, s], op0=ALU.add, op1=ALU.mult)
            link(m)
            link(nc.vector.tensor_reduce(pos[0:T, :], prefix[0:T, :].rearrange("p (t c) -> p c t", t=NT),
                                         AX.X, ALU.add))
            link(nc.vector.tensor_copy(pos_i[0:T, :], pos[0:T, :]))
            link(nc.vector.tensor_scalar(part_i[0:T, :], pos_i[0:T, :], P - 1, None, ALU.bitwise_and))
            link(nc.vector.tensor_scalar(pos_i[0:T, :], pos_i[0:T, :], 7, None, ALU.arith_shift_right))
            link(nc.vector.tensor_copy(part[0:T, :], part_i[0:T, :]))
            link(nc.vector.tensor_copy(pos[0:T, :], pos_i[0:T, :]))
            link(nc.vector.scalar_tensor_tensor(out=pos[0:T, :], in0=part[0:T, :], scalar=float(SC),
                                                in1=pos[0:T, :], op0=ALU.mult, op1=ALU.add))
            nc.vector.tensor_copy(addr[0:T, :], pos[0:T, :])
            dve.wait_ge(pool_consts, 4)
            nc.vector.tensor_copy(iota_t[:], iota_i[:])
            link(nc.vector.tensor_copy(slot0[:], slot0_i[:]))
            link(nc.vector.tensor_scalar(tile_f[:], slot0[:], end[0:1, 0:1], None, ALU.is_ge))
            for t in range(1, NT - 1):
                link(nc.vector.scalar_tensor_tensor(out=tile_f[:], in0=slot0[:], scalar=end[0:1, t:t + 1],
                                                    in1=tile_f[:], op0=ALU.is_ge, op1=ALU.add))
            nc.vector.tensor_copy(step_tile[:], tile_f[:])


def project(nc, sb_in, ident, eps, xq, Wq, bq, Wk, bk, Wv, bv, k_d, v_d,
            addr, pair, slots_d, slot_src, slot_dst, w_gate, w_up, w_down, wT_d,
            scattered):
    with phase(nc, [scattered], 16 * EC) as sem, ExitStack() as ph:
        sb = sb_in(ph)
        w_hi = sb("w_qkv_hi", [P, 3, KT, D], F32R)
        w_lo = sb("w_qkv_lo", [P, 3, KT, D], F32R)
        w = sb("w_qkv", [P, 3, KT, D])
        b = sb("b_qkv", [P, 3, D])
        stage_addr = sb("stage_addr", [P, SCAT], U32)
        stage_pair = sb("stage_pair", [P, SCAT, 2], I32)
        back = sb("back", [P, SC, 2], I32)
        stats = sb("stats", [P, 2, 6])
        mv = sb("mv", [P, 2, 2])
        std = sb("std", [P, 2, 1])
        rstd = sb("rstd", [P, 2, 1])
        y = sb("y", [P, 2, D])
        yT_hi = sb("yT_hi1", [P, 2, KT * T], F32R)
        yT_lo = sb("yT_lo1", [P, 2, KT * T], F32R)
        kv = sb("kv", [P, 2, 2, D])
        psT = ph.enter_context(nc.psum_tensor("psT1", [P, 2, 512], F32))
        psM = ph.enter_context(nc.psum_tensor("psM1", [P, 3, 512], F32))
        w_in = [sem(f"wqkv_in{n}") for n in range(3)]
        b_in, chain, carrier = sem("bqkv_in"), sem("p1_chain"), sem("p1_carrier")
        staged, turn, baclanded = sem("staged"), sem("deal_turn"), sem("baclanded")
        whi_ready, wlo_ready, var_ready, std_ready, y_ready, yT_psum, hi_ready, lo_ready, m_ready, added = (
            sem("p1_" + n) for n in ("whi_ready", "wlo_ready", "var_ready", "std_ready", "y_ready", "yT_psum",
                                     "hi_ready", "lo_ready", "m_ready", "added"))
        kv_out = [sem("p1_kv_out0"), sem("p1_kv_out1")]
        ternary = Ternary(nc, sem, sb, ph, ident, w_gate, w_up, w_down, wT_d)
        block = ph.enter_context(nc.Block())

        @block.sync
        def _(sp):
            for n, W in enumerate((Wq, Wk, Wv)):
                sp.dma_start(w[:, n], W.rearrange("(k p) n -> p k n", p=P)).then_inc(w_in[n], 16)
            for n, v in enumerate((bq, bk, bv)):
                sp.dma_start(b[:, n, :], v.rearrange("(o n) -> o n", o=1).to_broadcast([P, D])).then_inc(b_in, 16)

            def store(i, s):
                sp.wait_ge(added, 3 * i + 6)
                sp.dma_start(k_d[rows(i), :], kv[0:T, s, 0, :]).then_inc(kv_out[s], 16)
                sp.dma_start(v_d[rows(i), :], kv[0:T, s, 1, :]).then_inc(kv_out[s], 16)

            over(sp, NT, (0, store))
            ternary.loads_and_stores(sp)
            sp.wait_ge(kv_out[0], 32 * (NT // 2 + 2))
            sp.wait_ge(kv_out[1], 32 * (NT // 2 + 1))
            sp.wait_ge(scattered, 16 * EC)
            sp.dma_start(back[:], slots_d.rearrange("(p c) two -> p c two", p=P)).then_inc(baclanded, 16)

        @block.gpsimd
        def _(pool):
            def scatter(i):
                nc.gpsimd.tensor_copy(stage_addr[0:T, :], addr[0:T, bass.ds(i * SCAT, SCAT)]).then_inc(staged, 1)
                nc.gpsimd.tensor_copy(stage_pair[0:T], pair[0:T, bass.ds(i * SCAT, SCAT), :]).then_inc(staged, 1)
                pool.wait_ge(staged, 2 * i + 2)
                pool.sem_inc(turn, 1)
                for j in range(SCAT):
                    nc.gpsimd.indirect_dma_start(
                        slots_d, bass.IndirectOffsetOnAxis(ap=stage_addr[0:T, j:j + 1], axis=0),
                        stage_pair[0:T, j, :], None).then_inc(scattered, 16)

            scatter(0)
            with pool.Fori(1, EC // SCAT) as i:
                pool.wait_ge(scattered, 16 * SCAT * i)
                pool.sem_inc(turn, 1)
                scatter(i)

        @block.vector
        def _(dve):
            dve.sem_inc(y_ready, 2)
            dve.sem_inc(lo_ready, 2)
            dve.sem_inc(added, 3)
            dve.sem_inc(kv_out[0], 32)
            dve.sem_inc(kv_out[1], 32)
            for n in range(3):
                dve.wait_ge(whi_ready, n + 1)
                nc.vector.tensor_tensor(w_lo[:, n], w[:, n], w_hi[:, n].bitcast(F32),
                                        ALU.subtract).then_inc(wlo_ready, 1)
            dve.wait_ge(b_in, 48)
            c = Chain(dve, chain, 2)

            def normalize(i, s):
                c.start(i)
                xt = xq[0:T, bass.ds(i * D, D)]
                c.link(nc.vector.bn_stats(stats[0:T, s, :], xt))
                dve.sem_inc(carrier, 1)
                nc.vector.bn_aggr(mv[0:T, s, :], stats[0:T, s, :]).then_inc(var_ready, 1)
                dve.wait_ge(std_ready, i + 1)
                c.link(nc.vector.reciprocal(rstd[0:T, s, :], std[0:T, s, :]))
                dve.wait_ge(yT_psum, i + 1)
                nc.vector.tensor_scalar(y[0:T, s, :], xt, mv[0:T, s, 0:1], rstd[0:T, s, 0:1],
                                        ALU.subtract, ALU.mult).then_inc(y_ready, 1)
                c.end()

            def low(i, s):
                dve.wait_ge(hi_ready, i + 1)
                nc.vector.tensor_tensor(yT_lo[:, s, :], psT[:, s, 0:KT * T], yT_hi[:, s, :].bitcast(F32),
                                        ALU.subtract).then_inc(lo_ready, 1)

            def add_biases(i, s):
                dve.wait_ge(m_ready, 3 * i + 7)
                nc.vector.tensor_tensor(xq[0:T, bass.ds(i * D, D)], psM[0:T, 0, :], b[0:T, 0, :],
                                        ALU.add).then_inc(added, 1)
                dve.wait_ge(kv_out[s], 2 * lap(i, s))
                for n in (1, 2):
                    dve.wait_ge(m_ready, 3 * i + 7 + n)
                    nc.vector.tensor_tensor(kv[0:T, s, n - 1], psM[0:T, n, :], b[0:T, n, :],
                                            ALU.add).then_inc(added, 1)

            over(dve, NT, (0, normalize), (1, low), (2, add_biases))
            ternary.quantize(dve)
            dve.wait_ge(baclanded, 16)
            nc.vector.tensor_copy(slot_src[:, 0:SC].rearrange("p (c o) -> p c o", o=1), back[:, :, 0:1])
            nc.vector.tensor_copy(slot_dst[:, 0:SC].rearrange("p (c o) -> p c o", o=1), back[:, :, 1:2])

        @block.scalar
        def _(act):
            def root(i, s):
                act.wait_ge(var_ready, i + 1)
                nc.scalar.activation(std[0:T, s, :], mv[0:T, s, 1:2], ACT.Sqrt,
                                     bias=eps[0:T, :]).then_inc(std_ready, 1)

            def turn(i, s):
                act.wait_ge(yT_psum, i + 3)
                act.wait_ge(m_ready, 3 * i + 3)
                nc.scalar.copy(yT_hi[:, s, :], psT[:, s, 0:KT * T]).then_inc(hi_ready, 1)

            for n in range(3):
                act.wait_ge(w_in[n], 16)
                nc.scalar.copy(w_hi[:, n], w[:, n]).then_inc(whi_ready, 1)
            over(act, NT, (0, root), (1, turn))
            ternary.place(act)

        @block.tensor
        def _(pe):
            pe.sem_inc(yT_psum, 2)
            pe.sem_inc(m_ready, 6)

            def transposes(i, s):
                pe.wait_ge(y_ready, i + 3)
                pe.wait_ge(lo_ready, i + 1)
                for k in range(KT):
                    t = nc.tensor.transpose(psT[:, s, k * T:(k + 1) * T], y[0:T, s, k * P:(k + 1) * P],
                                            ident[0:T, 0:T])
                t.then_inc(yT_psum, 1)

            def products(i, s):
                if isinstance(i, int) and i == 0:
                    pe.wait_ge(wlo_ready, 3)
                pe.wait_ge(lo_ready, i + 3)
                for n in range(3):
                    pe.wait_ge(added, 3 * i + n + 1)
                    for k in range(KT):
                        c = slice(k * T, (k + 1) * T)
                        t = product3(nc, psM[0:T, n, :], (yT_hi[:, s, c], yT_lo[:, s, c]),
                                     (w_hi[:, n, k, :], w_lo[:, n, k, :]), k == 0, k == KT - 1)
                    t.then_inc(m_ready, 1)

            over(pe, NT, (0, transposes), (1, products))
            ternary.transpose(pe)


def chunk_pair(t, s, width):
    return t[:, bass.ds(s * 2 * width, 2 * width)].rearrange("p (c w) -> p c w", c=2)


def distances(nc, off, iota_t, slot_dst, s, b):
    for h in range(2):
        t = nc.scalar.activation(off[:, b, h, :], iota_t[:], ACT.Abs, scale=-1.0,
                                 bias=slot_dst[:, bass.ds(s * 2 + h, 1)])
    return t


def onehots(nc, oh, off, b):
    return nc.scalar.activation(oh[:, b], off[:, b], ACT.Relu, scale=-1.0, bias=1.0)


def stage_index(nc, act, slot_src, index, i, u, consumed, index_ready):
    act.wait_ge(consumed, i + u + RING)
    nc.scalar.copy(index[:, u // RING % 2, :], slot_src[:, bass.ds((i + u) * 2, 2 * RING)]).then_inc(index_ready, 1)


def gather_steps(nc, pool, rows_d, index, index_ready, buf, consumed, turn, landed):
    with pool.Fori(0, NS - U + 1, U) as i:
        for u in range(U):
            if u % RING == 0:
                pool.wait_ge(index_ready, i // RING + u // RING + 1)
                pool.sem_inc(turn, 1)
            pool.wait_ge(consumed, i + u + RING + 1)
            pool.sem_inc(turn, 1)
            for h in range(2):
                col = 2 * (u % RING) + h
                nc.gpsimd.indirect_dma_start(
                    buf[:, u % RING, h * D:(h + 1) * D], None, rows_d,
                    bass.IndirectOffsetOnAxis(ap=index[:, u // RING, col:col + 1], axis=0)
                ).then_inc(landed[u % RING], 16)


def score_pass(nc, sb_in, ident, iota_t, slot_src, slot_dst, step_tile, e9, q_sb, k_d, landed):
    with phase(nc, landed, 32 * NS // RING) as sem, ExitStack() as ph:
        sb = sb_in(ph)
        index = sb("landeddex", [P, 2, 2 * RING], U32)
        krows = sb("krows", [P, RING, 2 * D])
        off = sb("off2", [P, 2, 2, T])
        oh = sb("oh2", [P, 2, 2, T])
        ohT = sb("ohT", [P, 2, 2 * P])
        prod = sb("prod", [P, RING, 2 * D])
        psT = ph.enter_context(nc.psum_tensor("psT2", [P, 2, 512], F32))
        psQ = ph.enter_context(nc.psum_tensor("psQ2", [P, 2, 1024], F32))
        index_ready, turn, off_ready, oh_ready, ohT_psum, ohT_ready, q_ready, scored, reduced = (
            sem("p2_" + n) for n in ("index_ready", "turn", "off_ready", "oh_ready", "ohT_psum", "ohT_ready",
                                     "q_ready", "scored", "reduced"))
        block = ph.enter_context(nc.Block())

        @block.gpsimd
        def _(pool):
            gather_steps(nc, pool, k_d, index, index_ready, krows, scored, turn, landed)

        @block.scalar
        def _(act):
            act.sem_inc(ohT_ready, 2)

            def turn_onehots(s, b):
                act.wait_ge(ohT_psum, s + 3)
                act.wait_ge(q_ready, s + 1)
                nc.scalar.copy(ohT[0:T, b, :], psT[0:T, b, 0:2 * P]).then_inc(ohT_ready, 1)

            stage_index(nc, act, slot_src, index, 0, 0, scored, index_ready)
            for b in range(2):
                distances(nc, off, iota_t, slot_dst, b, b).then_inc(off_ready, 1)
                act.wait_ge(off_ready, b + 1)
                onehots(nc, oh, off, b).then_inc(oh_ready, 1)
            turn_onehots(0, 0)
            with act.Fori(0, NS - U + 1, U) as i:
                for u in range(U):
                    if u % RING == 0:
                        stage_index(nc, act, slot_src, index, i, u + RING, scored, index_ready)
                    distances(nc, off, iota_t, slot_dst, i + u + 2, u % 2).then_inc(off_ready, 1)
                    turn_onehots(i + u + 1, (u + 1) % 2)
                    act.wait_ge(off_ready, i + u + 3)
                    onehots(nc, oh, off, u % 2).then_inc(oh_ready, 1)

        @block.tensor
        def _(pe):
            pe.sem_inc(ohT_psum, 2)
            pe.sem_inc(q_ready, 2)

            def transposes(s, b):
                pe.wait_ge(oh_ready, s + 1)
                pe.wait_ge(ohT_ready, s + 1)
                for h in range(2):
                    t = nc.tensor.transpose(psT[0:T, b, h * P:(h + 1) * P], oh[:, b, h, :], ident[:])
                t.then_inc(ohT_psum, 1)

            transposes(0, 0)
            with pe.Fori(0, NS - U + 1, U) as i:
                for u in range(U):
                    s, b = i + u, u % 2
                    transposes(s + 1, (u + 1) % 2)
                    tile = pe.value_load(step_tile[0:1, bass.ds(s, 1)], min_val=0, max_val=NT - 1)
                    pe.wait_ge(ohT_ready, s + 3)
                    pe.wait_ge(scored, s + RING + 3)
                    for h in range(2):
                        t = nc.tensor.matmul(psQ[:, b, h * D:(h + 1) * D], ohT[0:T, b, h * P:(h + 1) * P],
                                             q_sb[0:T, bass.ds(tile * D, D)], start=True, stop=True)
                    t.then_inc(q_ready, 1)

        @block.vector
        def _(dve):
            dve.sem_inc(scored, 2 * RING)
            dve.sem_inc(reduced, RING)

            def multiply(i, u):
                s, r = i + u, u % RING
                dve.wait_ge(landed[r], i * (32 // RING) + 32 * (u // RING + 1))
                dve.wait_ge(q_ready, s + 3)
                dve.wait_ge(reduced, s + 1)
                nc.vector.tensor_tensor(prod[:, r, :], psQ[:, u % 2, :], krows[:, r, :], ALU.mult).then_inc(scored, 1)

            def reduce(i, u):
                s = i + u
                dve.wait_ge(scored, s + 2 * RING + 1)
                nc.vector.tensor_reduce(chunk_pair(e9, s, H + 1)[:, :, 0:H],
                                        prod[:, u % RING, :].rearrange("p (c h d) -> p c h d", c=2, h=H),
                                        AX.X, ALU.add).then_inc(reduced, 1)

            with dve.Fori(0, NS - U + 1, U) as i:
                for u in range(U):
                    multiply(i, u)
                    if u:
                        reduce(i, u - 1)
                reduce(i, U - 1)


def softmax_weights(nc, sb_in, slot_dst, e9, acc):
    with phase(nc) as sem, ExitStack() as ph:
        sb = sb_in(ph)
        empty = sb("empty", [P, SC])
        most = sb("most", [P, 1])
        top = sb("top", [P, 1])
        shift = sb("shift", [P, 1])
        chain, most_ready, top_ready, shift_ready = sem("p3_chain"), sem("most"), sem("top"), sem("shift")
        half = NT // 2 * AW
        scores = e9[:].rearrange("p (c w) -> p c w", w=H + 1)[:, :, 0:H]
        block = ph.enter_context(nc.Block())

        @block.vector
        def _(dve):
            c = Chain(dve, chain)
            c.link(nc.vector.tensor_scalar(empty[:], slot_dst[:, 0:SC], 0.0, -1e30, ALU.is_lt, ALU.mult))
            c.link(nc.vector.tensor_tensor(
                scores, scores, empty[:].rearrange("p (c w) -> p c w", w=1).to_broadcast([P, SC, H]), ALU.add))
            nc.vector.tensor_reduce(most[:], scores, AX.XY, ALU.max).then_inc(most_ready, 1)
            dve.wait_ge(top_ready, 1)
            nc.vector.tensor_scalar(shift[:], top[:], -(DH ** -0.5), 3.0, ALU.mult, ALU.add).then_inc(shift_ready, 1)
            nc.vector.memset(acc[:, half:], 0.0)

        @block.gpsimd
        def _(pool):
            nc.gpsimd.memset(acc[:, :half], 0.0)
            pool.wait_ge(most_ready, 1)
            nc.gpsimd.partition_all_reduce(top[:], most[:], P, bass.bass_isa.ReduceOp.max).then_inc(top_ready, 1)

        @block.scalar
        def _(act):
            act.wait_ge(shift_ready, 1)
            nc.scalar.activation(scores, scores, ACT.Exp, bias=shift[:], scale=DH ** -0.5)


def aggregate(nc, sb_in, name, iota_t, slot_src, slot_dst, step_tile, rows_d, acc, e9, landed):
    width = AW if e9 is not None else D
    with phase(nc, landed, 32 * NS // RING) as sem, ExitStack() as ph:
        sb = sb_in(ph)
        index = sb(name + "_index", [P, 2, 2 * RING], U32)
        got = sb(name + "_rows", [P, RING, 2 * D])
        off = sb(name + "_off", [P, 2, 2, T])
        oh = sb(name + "_oh", [P, 2, 2, T])
        msg = sb(name + "_msg", [P, RING, 2 * D]) if e9 is not None else None
        ps = ph.enter_context(nc.psum_tensor(name + "_ps", [P, 2, 1024], F32))
        index_ready, turn, off_ready, oh_ready, msg_ready, summed, added = (
            sem(f"{name}_{n}") for n in ("index_ready", "turn", "off_ready", "oh_ready", "msg_ready", "summed",
                                         "added"))
        used = summed if e9 is None else msg_ready
        block = ph.enter_context(nc.Block())

        @block.gpsimd
        def _(pool):
            gather_steps(nc, pool, rows_d, index, index_ready, got, used, turn, landed)

        @block.scalar
        def _(act):
            stage_index(nc, act, slot_src, index, 0, 0, used, index_ready)
            act.sem_inc(oh_ready, 1)
            distances(nc, off, iota_t, slot_dst, 0, 0).then_inc(off_ready, 1)
            with act.Fori(0, NS - U + 1, U) as i:
                for u in range(U):
                    if u % RING == 0:
                        stage_index(nc, act, slot_src, index, i, u + RING, used, index_ready)
                    act.wait_ge(oh_ready, i + u + 1)
                    distances(nc, off, iota_t, slot_dst, i + u + 1, (u + 1) % 2).then_inc(off_ready, 1)
                    act.wait_ge(off_ready, i + u + 1)
                    act.wait_ge(summed, i + u + 2 * RING - 1)
                    onehots(nc, oh, off, u % 2).then_inc(oh_ready, 1)

        def arrived(eng, i, u):
            eng.wait_ge(landed[u % RING], i * (32 // RING) + 32 * (u // RING + 1))

        def weigh(dve, i, u):
            if e9 is not None:
                s = i + u
                arrived(dve, i, u)
                dve.wait_ge(summed, s + RING + 1)
                nc.vector.tensor_tensor(
                    msg[:, u % RING, :].rearrange("p (c h d) -> p c h d", c=2, h=H),
                    got[:, u % RING, :].rearrange("p (c h d) -> p c h d", c=2, h=H),
                    chunk_pair(e9, s, H + 1)[:, :, 0:H].rearrange("p c (h o) -> p c h o", o=1).to_broadcast(
                        [P, 2, H, DH]), ALU.mult).then_inc(msg_ready, 1)

        @block.tensor
        def _(pe):
            pe.sem_inc(summed, 2 * RING)
            with pe.Fori(0, NS - U + 1, U) as i:
                for u in range(U):
                    s, b = i + u, u % 2
                    pe.wait_ge(oh_ready, s + 2)
                    if e9 is None:
                        arrived(pe, i, u)
                    else:
                        pe.wait_ge(msg_ready, s + 2 * RING + 1)
                    pe.wait_ge(added, s + 1)
                    for h in range(2):
                        rhs = (got if e9 is None else msg)[:, u % RING, h * D:(h + 1) * D]
                        t = nc.tensor.matmul(ps[0:T, b, 0:D], oh[:, b, h, :], rhs, start=(h == 0), stop=(h == 1))
                    if e9 is not None:
                        for h in range(2):
                            t = nc.tensor.matmul(ps[0:T, b, D:AW], oh[:, b, h, :],
                                                 e9[:, bass.ds((s * 2 + h) * (H + 1), H + 1)],
                                                 start=(h == 0), stop=(h == 1))
                    t.then_inc(summed, 1)

        @block.vector
        def _(dve):
            dve.sem_inc(added, 2)

            def add(i, u):
                s, b = i + u, u % 2
                tile = dve.value_load(step_tile[0:1, bass.ds(s, 1)], min_val=0, max_val=NT - 1)
                dve.wait_ge(added, s + 2)
                dve.wait_ge(summed, s + 2 * RING + 1)
                part = acc[0:T, bass.ds(tile * AW, width)]
                nc.vector.tensor_tensor(part, part, ps[0:T, b, 0:width], ALU.add).then_inc(added, 1)

            if e9 is not None:
                dve.sem_inc(msg_ready, 2 * RING)
            weigh(dve, 0, 0)
            weigh(dve, 0, 1)
            with dve.Fori(0, NS - 2 * U + 1, U) as i:
                for u in range(U):
                    weigh(dve, i, u + 2)
                    add(i, u)
            for u in range(U):
                if u < U - 2:
                    weigh(dve, NS - U, u + 2)
                add(NS - U, u)


def after_attention(nc, sb_in, ident, eps, x, Wff, bff, nibble_w, acc, dis, x2, g_d):
    feat_stack = ExitStack()
    sb = sb_in(feat_stack)
    nib = sb("nib", [P, NT, 4])
    marks = sb("marks", [P, NT, 3])
    opc = sb("opc", [P, NT, 2])
    attention_out(nc, sb_in, ident, eps, x, Wff, bff, acc, dis, x2, nib, marks, opc)
    res = sb("res", [P, NT, 2, 2, 2])
    nibble_pipelines(nc, sb_in, ident, nibble_w, nib, opc, res)
    alu_out(nc, sb_in, eps, marks, res, acc, dis, x2, g_d)
    feat_stack.close()


def attention_out(nc, sb_in, ident, eps, x, Wff, bff, acc, dis, x2, nib, marks, opc):
    with phase(nc) as sem, ExitStack() as ph:
        sb = sb_in(ph)
        w = sb("w_ff", [P, KT, D])
        b = sb("b_ff", [P, D])
        w16 = sb("w16", [P, 4 * 16])
        w16_i = sb("w16_i", [P, 4 * 16], I32)
        xt = sb("xt4", [P, 2, D])
        none = sb("none", [P, 2, H])
        rden = sb("rden", [P, 2, H])
        att = sb("att", [P, 2, D])
        attT = sb("attT", [P, 2, KT * T])
        x1 = sb("x1", [P, 2, D])
        y = sb("y4", [P, 2, D])
        stats = sb("stats4", [P, 2, 6])
        mv = sb("mv4", [P, 2, 2])
        std = sb("std4", [P, 2, 1])
        rstd = sb("rstd4", [P, 2, 1])
        bits = sb("bits", [P, 2, 64])
        psT = ph.enter_context(nc.psum_tensor("psT4", [P, 2, 512], F32))
        psM = ph.enter_context(nc.psum_tensor("psM4", [P, 2, 512], F32))
        w_in, w16_ready, chain, chain2, carrier, deg_sqrt = (
            sem("p4_" + n) for n in ("w_in", "w16_ready", "chain", "chain2", "carrier", "deg_sqrt"))
        x_in = [sem("p4_x_in0"), sem("p4_x_in1")]
        att_ready, attT_psum, attT_ready, m_ready, x1_ready, var_ready, std_ready = (
            sem("p4_" + n) for n in ("att_ready", "attT_psum", "attT_ready", "m_ready", "x1_ready", "var_ready",
                                     "std_ready"))
        tiles = acc[0:T, :].rearrange("p (t w) -> p t w", t=NT)
        block = ph.enter_context(nc.Block())

        @block.sync
        def _(sp):
            sp.dma_start(w[:], Wff.rearrange("(k p) n -> p k n", p=P)).then_inc(w_in, 16)
            sp.dma_start(b[:], bff.rearrange("(o n) -> o n", o=1).to_broadcast([P, D])).then_inc(w_in, 16)

            def load(i, s):
                sp.wait_ge(x1_ready, i + 1)
                sp.dma_start(xt[0:T, s, :], x[rows(i), :]).then_inc(x_in[s], 16)

            over(sp, NT, (0, load))

        @block.gpsimd
        def _(pool):
            nc.gpsimd.iota(w16_i[:], [[0, 4], [-1, 16]], base=16, channel_multiplier=0).then_inc(w16_ready, 1)

        @block.scalar
        def _(act):
            act.sem_inc(attT_ready, 2)
            act.wait_ge(deg_sqrt, 1)
            nc.scalar.activation(dis[0:T, :], dis[0:T, :], ACT.Sqrt).then_inc(deg_sqrt, 1)

            def turn(i, s):
                act.wait_ge(attT_psum, i + 3)
                act.wait_ge(m_ready, i + 1)
                nc.scalar.copy(attT[:, s, :], psT[:, s, 0:KT * T]).then_inc(attT_ready, 1)

            def root(i, s):
                act.wait_ge(var_ready, i + 1)
                nc.scalar.activation(std[0:T, s, :], mv[0:T, s, 1:2], ACT.Sqrt, bias=eps[0:T, :]).then_inc(std_ready, 1)

            over(act, NT, (0, turn), (1, root))

        @block.tensor
        def _(pe):
            pe.sem_inc(attT_psum, 2)
            pe.sem_inc(m_ready, 2)
            pe.wait_ge(w_in, 32)

            def transposes(i, s):
                pe.wait_ge(att_ready, i + 1)
                pe.wait_ge(attT_ready, i + 1)
                for k in range(KT):
                    t = nc.tensor.transpose(psT[:, s, k * T:(k + 1) * T], att[0:T, s, k * P:(k + 1) * P],
                                            ident[0:T, 0:T])
                t.then_inc(attT_psum, 1)

            def product(i, s):
                pe.wait_ge(attT_ready, i + 3)
                pe.wait_ge(x1_ready, i + 1)
                for k in range(KT):
                    t = nc.tensor.matmul(psM[0:T, s, :], attT[:, s, k * T:(k + 1) * T], w[:, k, :],
                                         start=(k == 0), stop=(k == KT - 1))
                t.then_inc(m_ready, 1)

            over(pe, NT, (0, transposes), (1, product))

        @block.vector
        def _(dve):
            dve.sem_inc(x1_ready, 2)
            c0 = Chain(dve, chain2)
            nc.vector.tensor_scalar(dis[0:T, :], tiles[:, :, AW - 1], 1.0, None, ALU.add).then_inc(deg_sqrt, 1)
            dve.wait_ge(w16_ready, 1)
            c0.link(nc.vector.tensor_copy(w16[:], w16_i[:]))
            dve.wait_ge(deg_sqrt, 2)
            c0.link(nc.vector.reciprocal(dis[0:T, :], dis[0:T, :]))
            dve.wait_ge(w_in, 32)
            done = c0.n
            c1, c2 = Chain(dve, chain, 3), Chain(dve, chain2, 5)

            def divide(i, s):
                c1.start(i)
                den = acc[0:T, bass.ds(i * AW + D, H)]
                c1.link(nc.vector.tensor_scalar(none[0:T, s, :], den, 0.0, None, ALU.is_equal))
                c1.link(nc.vector.tensor_tensor(rden[0:T, s, :], den, none[0:T, s, :], ALU.add))
                c1.link(nc.vector.reciprocal(rden[0:T, s, :], rden[0:T, s, :]))
                dve.wait_ge(attT_psum, i + 1)
                nc.vector.tensor_tensor(
                    att[0:T, s, :].rearrange("p (h d) -> p h d", h=H),
                    acc[0:T, bass.ds(i * AW, D)].rearrange("p (h d) -> p h d", h=H),
                    rden[0:T, s, :].rearrange("p (h o) -> p h o", o=1).to_broadcast([T, H, DH]),
                    ALU.mult).then_inc(att_ready, 1)
                c1.end()

            def residual(i, s):
                c2.start(i)
                c2.base = c2.base + done
                dve.wait_ge(x_in[s], lap(i, s))
                c2.link(nc.vector.tensor_tensor(xt[0:T, s, :], xt[0:T, s, :], b[0:T, :], ALU.add))
                dve.wait_ge(m_ready, i + 3)
                nc.vector.tensor_tensor(x1[0:T, s, :], psM[0:T, s, :], xt[0:T, s, :], ALU.add).then_inc(x1_ready, 1)
                dve.wait_ge(x1_ready, i + 3)
                c2.link(nc.vector.bn_stats(stats[0:T, s, :], x1[0:T, s, :]))
                dve.sem_inc(carrier, 1)
                nc.vector.bn_aggr(mv[0:T, s, :], stats[0:T, s, :]).then_inc(var_ready, 1)
                dve.wait_ge(std_ready, i + 1)
                c2.link(nc.vector.reciprocal(rstd[0:T, s, :], std[0:T, s, :]))
                c2.link(nc.vector.tensor_scalar(y[0:T, s, :], x1[0:T, s, :], mv[0:T, s, 0:1], rstd[0:T, s, 0:1],
                                                ALU.subtract, ALU.mult))
                c2.link(nc.vector.scalar_tensor_tensor(out=bits[0:T, s, :], in0=y[0:T, s, 16:80], scalar=0.5,
                                                       in1=w16[0:T, :], op0=ALU.is_gt, op1=ALU.mult))
                nc.vector.tensor_reduce(nib[0:T, bass.ds(i, 1), :],
                                        bits[0:T, s, :].rearrange("p (f o j) -> p f o j", f=1, j=16),
                                        AX.X, ALU.max)
                nc.vector.tensor_scalar(marks[0:T, bass.ds(i, 1), :],
                                        y[0:T, s, 0:3].rearrange("p (f j) -> p f j", f=1), 0.5, None, ALU.is_gt)
                nc.vector.tensor_copy(opc[0:T, bass.ds(i, 1), :],
                                      y[0:T, s, 105:107].rearrange("p (f j) -> p f j", f=1))
                nc.vector.tensor_tensor(x2[0:T, bass.ds(i * D, D)], x1[0:T, s, :], y[0:T, s, :], ALU.add)
                c2.end()

            over(dve, NT, (0, divide), (1, residual))


GE_PARTS = ((0, 0, P), (1, P, GE - P))


def nibble_weights(sb):
    return dict(w1=sb("w1", [P, 2, GE]), w2n=sb("w2n", [P, 2, 2, GE]),
                w2=sb("w2", [P, 2, 2, GE]),
                w3=sb("w3", [P, 2, 2, 2]),
                b2=sb("b2", [P, 2, 2]),
                b3=sb("b3", [P, 2, 2]))


def load_nibble_weights(nc, sp, weights, w_in, Wa, ba, Ws, bs):
    w1, w2n, w3, b2, b3 = (weights[k] for k in ("w1", "w2n", "w3", "b2", "b3"))
    with nc.allow_non_contiguous_dma(reason="a few columns of small weights"):
        for q, (W, bias) in enumerate(((Wa, ba), (Ws, bs))):
            for r, f in ((0, 0), (1, 1), (2, 35), (3, 36)):
                sp.dma_start(w1[r:r + 1, q, :], W[0, :, f:f + 1].rearrange("o d -> d o")).then_inc(w_in, 16)
            sp.dma_start(w1[4:5, q, :], bias[0:1, :]).then_inc(w_in, 16)
            for n, o, m in GE_PARTS:
                sp.dma_start(w2n[0:m, q, n, :], W[1, o:o + m, :]).then_inc(w_in, 16)
                sp.dma_start(w3[0:m, q, n, :], W[2, 100:102, o:o + m].rearrange("o d -> d o")).then_inc(w_in, 16)
                sp.dma_start(b2[0:m, q, n:n + 1], bias[1:2, o:o + m].rearrange("o d -> d o")).then_inc(w_in, 16)
            sp.dma_start(b3[:, q, :], bias[2:3, 100:102].to_broadcast([P, 2])).then_inc(w_in, 16)
    return 2 * (5 + 6 + 1)


def nibble_pipelines(nc, sb_in, ident, weights, nib, opc, res):
    G = 2
    C = G * 2 * T
    NG = -(-NT // G)

    def tiles_of(g):
        return NT - (NG - 1) * G if isinstance(g, int) and g == NG - 1 else G

    with phase(nc) as sem, ExitStack() as ph:
        sb = sb_in(ph)
        set_ = sb("nib_set", [P, NT, 4])
        val = sb("nib_val", [P, NT, 4])
        feat = sb("feat", [P, NT + 1, 2, 5])
        w1, w2, w3, b2, b3 = (weights[k] for k in ("w1", "w2", "w3", "b2", "b3"))
        fst = sb("fst", [P, 2, G * 2, 5])
        fT = sb("fT", [P, 2, C])
        h1 = sb("h1", [P, 2, 2, 2, C])
        h2 = sb("h2", [P, 2, 2, C])
        psF = ph.enter_context(nc.psum_tensor("psF", [P, 512], F32))
        ps1 = ph.enter_context(nc.psum_tensor("ps1", [P, 2, 2, 512], F32))
        ps2 = ph.enter_context(nc.psum_tensor("ps2", [P, 2, 512], F32))
        ps3 = ph.enter_context(nc.psum_tensor("ps3", [P, 512], F32))
        chain = sem("p5_chain")
        staged, f_psum, f_ready, l1, r1, l2, r2, l3, r3 = (
            sem("p5_" + n) for n in ("staged", "f_psum", "f_ready", "l1", "r1", "l2", "r2", "l3", "r3"))
        block = ph.enter_context(nc.Block())

        @block.vector
        def _(dve):
            c = Chain(dve, chain)
            c.link(nc.vector.memset(feat[:], 1.0))
            c.link(nc.vector.tensor_scalar(set_[0:T], nib[0:T], 0.0, None, ALU.is_gt))
            c.link(nc.vector.tensor_scalar(val[0:T], nib[0:T], -1.0, 16.0, ALU.mult, ALU.add))
            c.link(nc.vector.tensor_tensor(val[0:T], val[0:T], set_[0:T], ALU.mult))
            for a in range(2):
                c.link(nc.vector.tensor_copy(feat[0:T, 0:NT, :, a], val[0:T, :, 2 * a:2 * a + 2]))
            for p in range(2):
                c.link(nc.vector.tensor_copy(feat[0:T, 0:NT, p, 2:4], opc[0:T]))
            def stage(g, s):
                dve.wait_ge(f_psum, g + 1)
                k = tiles_of(g)
                nc.vector.tensor_copy(fst[0:T, s, 0:k * 2, :].rearrange("p (t q) f -> p t (q f)", q=2),
                                      feat[0:T, bass.ds(g * G, k), :, :].rearrange("p t q f -> p t (q f)")
                                      ).then_inc(staged, 1)

            def results(g, s):
                dve.wait_ge(l3, g + 1)
                k = tiles_of(g)
                for q in range(2):
                    for p in range(2):
                        o = (q * 2 + p) * G * 2
                        t = nc.vector.tensor_tensor(
                            res[0:T, bass.ds(g * G, k), q, p, :],
                            ps3[0:T, o:o + k * 2].rearrange("p (t r) -> p t r", t=k),
                            b3[0:T, q, :].rearrange("p (o r) -> p o r", o=1).to_broadcast([T, k, 2]), ALU.add)
                t.then_inc(r3, 1)

            over(dve, NG, (0, stage), (3, results), peel=1)

        @block.scalar
        def _(act):
            def features(g, s):
                act.wait_ge(f_psum, g + 3)
                act.wait_ge(l1, g + 1)
                cols = tiles_of(g) * 2 * T
                nc.scalar.copy(fT[0:5, s, 0:cols], psF[0:5, 0:cols]).then_inc(f_ready, 1)

            def layer1(g, s):
                act.wait_ge(l1, g + 3)
                cols = tiles_of(g) * 2 * T
                for q in range(2):
                    for n, o, m in GE_PARTS:
                        t = nc.scalar.activation(h1[0:m, s, q, n, 0:cols], ps1[0:m, q, n, 0:cols], ACT.Relu)
                t.then_inc(r1, 1)

            def layer2(g, s):
                cols = tiles_of(g) * 2 * T
                for q in range(2):
                    act.wait_ge(l2, 2 * g + q + 1)
                    for n, o, m in GE_PARTS:
                        t = nc.scalar.activation(h2[0:m, q, n, 0:cols], ps2[0:m, n, 0:cols], ACT.Relu,
                                                 bias=b2[0:m, q, n:n + 1])
                    t.then_inc(r2, 1)

            over(act, NG, (0, features), (1, layer1), (2, layer2), peel=1)

        @block.tensor
        def _(pe):
            pe.sem_inc(f_psum, 2)
            pe.sem_inc(l1, 2)
            pe.sem_inc(f_ready, 1)
            pe.sem_inc(r1, 1)
            pe.sem_inc(r2, 1)
            pe.sem_inc(r3, 1)

            def features(g, s):
                pe.wait_ge(staged, g + 1)
                pe.wait_ge(f_ready, g + 1)
                for j in range(tiles_of(g) * 2):
                    t = nc.tensor.transpose(psF[0:5, j * T:(j + 1) * T], fst[0:T, s, j, :], ident[0:T, 0:T])
                t.then_inc(f_psum, 1)

            def layer1(g, s):
                pe.wait_ge(f_ready, g + 2)
                pe.wait_ge(r1, g + 1)
                cols = tiles_of(g) * 2 * T
                for q in range(2):
                    for n, o, m in GE_PARTS:
                        t = nc.tensor.matmul(ps1[0:m, q, n, 0:cols], w1[0:5, q, o:o + m], fT[0:5, s, 0:cols],
                                             start=True, stop=True)
                t.then_inc(l1, 1)

            def layers23(g, s):
                k = tiles_of(g)
                cols = k * 2 * T
                pe.wait_ge(r1, g + 2)
                for q in range(2):
                    pe.wait_ge(r2, 2 * g + q + 1)
                    for n, o, m in GE_PARTS:
                        for n1, o1, m1 in GE_PARTS:
                            t = nc.tensor.matmul(ps2[0:m, n, 0:cols], w2[0:m1, q, n1, o:o + m],
                                                 h1[0:m1, s, q, n1, 0:cols], start=(n1 == 0), stop=(n1 == 1))
                    t.then_inc(l2, 1)
                pe.wait_ge(r2, 2 * g + 3)
                pe.wait_ge(r3, g + 1)
                for q in range(2):
                    for p in range(2):
                        for j in range(k):
                            col = ((q * 2 + p) * G + j) * 2
                            for n, o, m in GE_PARTS:
                                t = nc.tensor.matmul(ps3[0:T, col:col + 2],
                                                     h2[0:m, q, n, (j * 2 + p) * T:(j * 2 + p + 1) * T],
                                                     w3[0:m, q, n, :], start=(n == 0), stop=(n == 1))
                t.then_inc(l3, 1)

            over(pe, NG, (0, features), (1, layer1), (2, layers23), peel=1)


def alu_out(nc, sb_in, eps, marks, res, acc, dis, x2, g_d):
    with phase(nc) as sem, ExitStack() as ph:
        sb = sb_in(ph)
        madd = sb("madd", [P, NT])
        msub = sb("msub", [P, NT])
        not_add = sb("not_add", [P, NT])
        twice = sb("twice", [P, NT])
        pick = sb("pick", [P, NT, 4])
        tmp = sb("tmp", [P, NT, 4])
        iota16_i = sb("iota16_i", [P, 16], I32)
        iota16 = sb("iota16", [P, 16])
        hot = sb("hot", [P, NT, 2, 16])
        carry = sb("carry", [P, NT])
        stats = sb("stats6", [P, 2, 6])
        mv = sb("mv6", [P, 2, 2])
        std = sb("std6", [P, 2, 1])
        rstd = sb("rstd6", [P, 2, 1])
        i_ready, chain, chain2, carrier, var_ready, std_ready, g_ready, g_out = (
            sem("p6_" + n) for n in ("iota_ready", "chain", "chain2", "carrier", "var_ready", "std_ready", "g_ready",
                                     "g_out"))
        block = ph.enter_context(nc.Block())

        @block.gpsimd
        def _(pool):
            nc.gpsimd.iota(iota16_i[:], [[1, 16]], base=0, channel_multiplier=0).then_inc(i_ready, 1)

        @block.sync
        def _(sp):
            def store(i, s):
                sp.wait_ge(g_ready, i + 1)
                sp.dma_start(g_d[rows(i), :], acc[0:T, bass.ds(i * AW, D)]).then_inc(g_out, 16)

            over(sp, NT, (0, store))
            sp.wait_ge(g_out, 16 * NT)

        @block.scalar
        def _(act):
            def root(i, s):
                act.wait_ge(var_ready, i + 1)
                nc.scalar.activation(std[0:T, s, :], mv[0:T, s, 1:2], ACT.Sqrt, bias=eps[0:T, :]).then_inc(std_ready, 1)

            over(act, NT, (0, root))

        @block.vector
        def _(dve):
            c = Chain(dve, chain)
            v = nc.vector
            m0, m1, m2 = (marks[0:T, :, j] for j in range(3))
            c.link(v.tensor_tensor(madd[0:T], m0, m1, ALU.mult))
            c.link(v.tensor_scalar(not_add[0:T], m1, -1.0, 1.0, ALU.mult, ALU.add))
            c.link(v.tensor_tensor(msub[0:T], m0, m2, ALU.mult))
            c.link(v.tensor_tensor(msub[0:T], msub[0:T], not_add[0:T], ALU.mult))
            for m, q, to in ((madd, 0, pick), (msub, 1, tmp)):
                c.link(v.tensor_tensor(to[0:T], res[0:T, :, q].rearrange("p t a b -> p t (a b)"),
                                       m[0:T].rearrange("p (t o) -> p t o", o=1).to_broadcast([T, NT, 4]), ALU.mult))
            c.link(v.tensor_tensor(pick[0:T], pick[0:T], tmp[0:T], ALU.add))
            c.link(v.tensor_tensor(twice[0:T], madd[0:T], msub[0:T], ALU.add))
            c.link(v.tensor_scalar(carry[0:T], pick[0:T, :, 3], 0.5, None, ALU.is_gt))
            c.link(v.tensor_tensor(carry[0:T], carry[0:T], twice[0:T], ALU.mult))
            c.link(v.tensor_scalar(twice[0:T], twice[0:T], 2.0, None, ALU.mult))
            c.link(v.tensor_scalar(pick[0:T], pick[0:T], 0.0, 15.0, ALU.max, ALU.min))
            c.link(v.tensor_scalar(pick[0:T], pick[0:T], RNE, None, ALU.add))
            c.link(v.tensor_scalar(pick[0:T], pick[0:T], -RNE, None, ALU.add))
            dve.wait_ge(i_ready, 1)
            c.link(v.tensor_copy(iota16[:], iota16_i[:]))
            for p in range(2):
                c.link(v.tensor_tensor(hot[0:T, :, p, :],
                                       iota16[0:T, :].rearrange("p (o j) -> p o j", o=1).to_broadcast([T, NT, 16]),
                                       pick[0:T, :, 2 * p:2 * p + 1].to_broadcast([T, NT, 16]), ALU.is_equal))
            c.link(v.tensor_tensor(hot[0:T].rearrange("p t a j -> p t (a j)"),
                                   hot[0:T].rearrange("p t a j -> p t (a j)"),
                                   twice[0:T].rearrange("p (t o) -> p t o", o=1).to_broadcast([T, NT, 32]), ALU.mult))
            x2t = x2[0:T, :].rearrange("p (t d) -> p t d", t=NT)
            c.link(v.tensor_tensor(x2t[:, :, 128:160], x2t[:, :, 128:160],
                                   hot[0:T].rearrange("p t a j -> p t (a j)"), ALU.add))
            c.link(v.tensor_tensor(x2t[:, :, 160], x2t[:, :, 160], carry[0:T], ALU.add))
            c2 = Chain(dve, chain2, 3)

            def stats_of(i, s):
                c2.start(i)
                c2.link(v.bn_stats(stats[0:T, s, :], x2[0:T, bass.ds(i * D, D)]))
                dve.sem_inc(carrier, 1)
                v.bn_aggr(mv[0:T, s, :], stats[0:T, s, :]).then_inc(var_ready, 1)
                dve.wait_ge(std_ready, i + 1)
                c2.link(v.reciprocal(rstd[0:T, s, :], std[0:T, s, :]))
                c2.link(v.tensor_tensor(rstd[0:T, s, :], rstd[0:T, s, :], dis[0:T, bass.ds(i, 1)], ALU.mult))
                v.tensor_scalar(acc[0:T, bass.ds(i * AW, D)], x2[0:T, bass.ds(i * D, D)], mv[0:T, s, 0:1],
                                rstd[0:T, s, 0:1], ALU.subtract, ALU.mult).then_inc(g_ready, 1)
                c2.end()

            over(dve, NT, (0, stats_of))


def product3(nc, out, a, b, start, stop):
    nc.tensor.matmul(out, a[0], b[1], start=start, stop=False)
    nc.tensor.matmul(out, a[1], b[0], start=False, stop=False)
    return nc.tensor.matmul(out, a[0], b[0], start=False, stop=stop)


def gcn_dense(nc, sb_in, n, ident, W, b, acc, dis, x2, g_d):
    last = n == 2
    with phase(nc) as sem, ExitStack() as ph:
        sb = sb_in(ph)
        w = sb(f"w_gcn{n}", [P, KT, D])
        w_hi = sb(f"w_hi{n}", [P, KT, D], F32R)
        w_lo = sb(f"w_lo{n}", [P, KT, D], F32R)
        bias = sb(f"b_gcn{n}", [P, D])
        z = sb(f"z{n}", [P, 2, D])
        z_hi = sb(f"z_hi{n}", [P, 2, KT * T], F32R)
        z_lo = sb(f"z_lo{n}", [P, 2, KT * T], F32R)
        h = sb(f"h_gcn{n}", [P, 2, D])
        psT = ph.enter_context(nc.psum_tensor(f"psTg{n}", [P, 2, 512], F32))
        psM = ph.enter_context(nc.psum_tensor(f"psMg{n}", [P, 2, 512], F32))
        w_in, whi_ready, wlo_ready, z_ready, zT_psum, hi_ready, lo_ready, m_ready, h_ready, g_ready = (
            sem(f"g{n}_{k}") for k in ("w_in", "whi_ready", "wlo_ready", "z_ready", "zT_psum", "hi_ready", "lo_ready",
                                       "m_ready", "h_ready", "g_ready"))
        g_out, carrier = [sem(f"g{n}_out0"), sem(f"g{n}_out1")], sem(f"g{n}_carrier")
        block = ph.enter_context(nc.Block())

        @block.sync
        def _(sp):
            sp.dma_start(w[:], W.rearrange("(k p) n -> p k n", p=P)).then_inc(w_in, 16)
            sp.dma_start(bias[:], b.rearrange("(o n) -> o n", o=1).to_broadcast([P, D])).then_inc(w_in, 16)

            def store(i, s):
                if last:
                    sp.wait_ge(g_ready, i + 1)
                    sp.dma_start(g_d[rows(i), :], h[0:T, s, :]).then_inc(g_out[s], 16)
                else:
                    sp.wait_ge(g_ready, i + 3)
                    sp.dma_start(g_d[rows(i), :], acc[0:T, bass.ds(i * AW, D)]).then_inc(g_out[s], 16)

            over(sp, NT, (0, store))
            granted = 16 if last else 0
            sp.wait_ge(g_out[0], 16 * (NT // 2 + 1) + granted)
            sp.wait_ge(g_out[1], 16 * (NT // 2) + granted)

        @block.gpsimd
        def _(pool):
            def take(i, s):
                pool.wait_ge(zT_psum, i + 1)
                pool.sem_inc(carrier, 1)
                nc.gpsimd.tensor_copy(z[0:T, s, :], acc[0:T, bass.ds(i * AW, D)]).then_inc(z_ready, 1)

            over(pool, NT, (0, take))

        @block.tensor
        def _(pe):
            pe.sem_inc(zT_psum, 2)
            pe.sem_inc(m_ready, 2)

            def transposes(i, s):
                pe.wait_ge(z_ready, i + 1)
                pe.wait_ge(lo_ready, i + 1)
                for k in range(KT):
                    t = nc.tensor.transpose(psT[:, s, k * T:(k + 1) * T], z[0:T, s, k * P:(k + 1) * P],
                                            ident[0:T, 0:T])
                t.then_inc(zT_psum, 1)

            def product(i, s):
                if isinstance(i, int) and i == 0:
                    pe.wait_ge(wlo_ready, 1)
                pe.wait_ge(lo_ready, i + 3)
                pe.wait_ge(h_ready, i + 1)
                for k in range(KT):
                    c = slice(k * T, (k + 1) * T)
                    t = product3(nc, psM[0:T, s, :], (z_hi[:, s, c], z_lo[:, s, c]), (w_hi[:, k, :], w_lo[:, k, :]),
                                 k == 0, k == KT - 1)
                t.then_inc(m_ready, 1)

            over(pe, NT, (0, transposes), (1, product))

        @block.scalar
        def _(act):
            if not last:
                act.sem_inc(g_ready, 2)
            act.wait_ge(w_in, 32)
            nc.scalar.copy(w_hi[:], w[:]).then_inc(whi_ready, 1)

            def high(i, s):
                act.wait_ge(zT_psum, i + 3)
                act.wait_ge(m_ready, i + 1)
                nc.scalar.copy(z_hi[:, s, :], psT[:, s, 0:KT * T]).then_inc(hi_ready, 1)

            def rectify(i, s):
                if not last:
                    act.wait_ge(h_ready, i + 3)
                    nc.scalar.activation(acc[0:T, bass.ds(i * AW, D)], h[0:T, s, :], ACT.Relu,
                                         scale=dis[0:T, bass.ds(i, 1)]).then_inc(g_ready, 1)

            over(act, NT, (0, high), (2, rectify))

        @block.vector
        def _(dve):
            dve.sem_inc(h_ready, 2)
            dve.sem_inc(lo_ready, 2)
            if last:
                dve.sem_inc(g_out[0], 16)
                dve.sem_inc(g_out[1], 16)
            dve.wait_ge(whi_ready, 1)
            nc.vector.tensor_tensor(w_lo[:], w[:], w_hi[:].bitcast(F32), ALU.subtract).then_inc(wlo_ready, 1)

            def low(i, s):
                dve.wait_ge(hi_ready, i + 1)
                nc.vector.tensor_tensor(z_lo[:, s, :], psT[:, s, 0:KT * T], z_hi[:, s, :].bitcast(F32),
                                        ALU.subtract).then_inc(lo_ready, 1)

            def add_bias(i, s):
                dve.wait_ge(m_ready, i + 3)
                if last:
                    dve.wait_ge(g_out[s], lap(i, s))
                else:
                    dve.wait_ge(g_ready, i + 1)
                nc.vector.scalar_tensor_tensor(out=h[0:T, s, :], in0=psM[0:T, s, :], scalar=dis[0:T, bass.ds(i, 1)],
                                               in1=bias[0:T, :], op0=ALU.mult, op1=ALU.add).then_inc(h_ready, 1)
                if last:
                    dve.wait_ge(h_ready, i + 3)
                    nc.vector.tensor_tensor(h[0:T, s, :], h[0:T, s, :], x2[0:T, bass.ds(i * D, D)],
                                            ALU.add).then_inc(g_ready, 1)

            over(dve, NT, (0, low), (1, add_bias))


class Ternary:

    PG = 4

    def __init__(self, nc, sem, sb, ph, ident, w_gate, w_up, w_down, wT_d):
        self.nc, self.ident = nc, ident
        self.runs = [(w_gate, wT_d[0], 0, KT, FT), (w_up, wT_d[1], 0, KT, FT)]
        self.runs += [(w_down, wT_d[2], g, min(self.PG, FT - g), KT) for g in range(0, FT, self.PG)]
        self.pieces = sum(r[4] for r in self.runs)
        wide = self.PG * P
        self.w, self.wT = sb("t_w", [P, 2, wide]), sb("t_wT", [P, 2, wide])
        self.up, self.down = sb("t_up", [P, wide]), sb("t_down", [P, wide])
        self.total, self.scale, self.half, self.nhalf = (sb(f"t_{k}", [P, self.PG]) for k in
                                                         ("total", "scale", "half", "nhalf"))
        self.ps = ph.enter_context(nc.psum_tensor("t_ps", [P, 2, 512], F32))
        self.chain, self.quantized, self.turned, self.placed, self.carrier, self.blank = (
            sem("t_" + k) for k in ("chain", "quantized", "turned", "placed", "carrier", "blank"))
        self.w_in, self.w_out = [sem("t_in0"), sem("t_in1")], [sem("t_out0"), sem("t_out1")]

    def each(self, eng, *stages):
        first = 0
        for run in self.runs:
            over(eng, run[4], *((lag, lambda m, s, f=f, k=first, run=run: f(m + k, (s + k) % 2, run, m))
                                for lag, f in stages))
            first += run[4]

    def loads_and_stores(self, sp):
        sp.sem_inc(self.turned, 2)

        def load(n, s, run, m):
            src, _, g0, groups, _ = run
            sp.wait_ge(self.turned, n + 1)
            sp.sem_inc(self.carrier, 1)
            sp.dma_start(self.w[:, s, 0:groups * P],
                         src[bass.ds(m * P, P), g0 * P:(g0 + groups) * P]).then_inc(self.w_in[s], 16)

        def store(n, s, run, m):
            _, dst, g0, groups, _ = run
            sp.wait_ge(self.placed, n + 3)
            sp.sem_inc(self.carrier, 1)
            sp.dma_start(dst[:, g0:g0 + groups, bass.ds(m * P, P)],
                         self.wT[:, s, 0:groups * P].rearrange("p (g k) -> p g k", g=groups)
                         ).then_inc(self.w_out[s], 16)

        self.each(sp, (0, load), (1, store))
        sp.wait_ge(self.w_out[0], 16 * ((self.pieces + 1) // 2 + 1))
        sp.wait_ge(self.w_out[1], 16 * (self.pieces // 2 + 1))

    def quantize(self, dve):
        v = self.nc.vector
        c = Chain(dve, self.chain, 7)

        def piece(n, s, run, m):
            groups = run[3]
            c.start(n)
            dve.wait_ge(self.w_in[s], lap(n, s))
            wt, ut, dt = self.w[:, s, 0:groups * P], self.up[:, 0:groups * P], self.down[:, 0:groups * P]
            c.link(v.tensor_reduce(self.total[:, 0:groups], wt.rearrange("p (g k) -> p g k", g=groups), AX.X,
                                   ALU.add, apply_absolute_value=True))
            c.link(v.tensor_scalar(self.scale[:], self.total[:], 1.0 / P, EPS, ALU.mult, ALU.add))
            v.tensor_scalar(self.half[:], self.scale[:], 0.5, None, ALU.mult)
            c.link(v.tensor_scalar(self.nhalf[:], self.scale[:], -0.5, None, ALU.mult))
            for g in range(groups):
                k = slice(g * P, (g + 1) * P)
                v.tensor_scalar(self.up[:, k], self.w[:, s, k], self.half[:, g:g + 1], self.scale[:, g:g + 1],
                                ALU.is_gt, ALU.mult)
                t = v.tensor_scalar(self.down[:, k], self.w[:, s, k], self.nhalf[:, g:g + 1],
                                    self.scale[:, g:g + 1], ALU.is_lt, ALU.mult)
            c.link(t)
            c.link(v.tensor_tensor(ut, ut, dt, ALU.subtract))
            c.link(v.tensor_tensor(ut, ut, wt, ALU.subtract))
            c.link(v.tensor_tensor(wt, wt, ut, ALU.add))
            dve.sem_inc(self.quantized, 1)
            c.end()

        v.memset(self.total[:], 0.0).then_inc(self.blank, 1)
        dve.wait_ge(self.blank, 1)
        self.each(dve, (0, piece))

    def transpose(self, pe):
        def piece(n, s, run, m):
            pe.wait_ge(self.quantized, n + 1)
            pe.wait_ge(self.placed, n + 1)
            for g in range(run[3]):
                t = self.nc.tensor.transpose(self.ps[:, s, g * P:(g + 1) * P], self.w[:, s, g * P:(g + 1) * P],
                                             self.ident[:])
            t.then_inc(self.turned, 1)

        self.each(pe, (0, piece))

    def place(self, act):
        act.sem_inc(self.placed, 2)
        act.sem_inc(self.w_out[0], 16)
        act.sem_inc(self.w_out[1], 16)

        def piece(n, s, run, m):
            act.wait_ge(self.turned, n + 3)
            act.wait_ge(self.w_out[s], lap(n, s))
            wide = run[3] * P
            self.nc.scalar.copy(self.wT[:, s, 0:wide], self.ps[:, s, 0:wide]).then_inc(self.placed, 1)

        self.each(act, (0, piece))


def swiglu(nc, sb_in, ident, eps, wT_d, x3_d, out):
    G = 3
    C = G * T + G * T % 2
    NG = NT // G
    with phase(nc) as sem, ExitStack() as ph:
        sb = sb_in(ph)
        wT = [[sb(f"w{k}T_{part}", shape, F32R) for part in ("hi", "lo")]
              for k, shape in (("g", [P, KT, FF]), ("u", [P, KT, FF]), ("d", [P, FT, D]))]
        xt = sb("xt8", [P, G, D])
        xr = sb("xr8", [P, G, D])
        stats = sb("stats8", [P, G, 6])
        mv = sb("mv8", [P, G, 2])
        std = sb("std8", [P, G])
        yT = [sb("yT_hi", [P, KT, C], F32R), sb("yT_lo", [P, KT, C], F32R)]
        sg = sb("sg", [P, 2, C])
        hid = sb("hid", [P, 2, C])
        hT = [sb("hT_hi", [P, FT, C], F32R), sb("hT_lo", [P, FT, C], F32R)]
        psT = ph.enter_context(nc.psum_tensor("psT8", [P, 512], F32))
        psG = ph.enter_context(nc.psum_tensor("psG", [P, 2, 512], F32))
        psU = ph.enter_context(nc.psum_tensor("psU", [P, 2, 512], F32))
        psD = ph.enter_context(nc.psum_tensor("psD", [P, G, 512], F32))
        x_in, r_in, o_out = ([sem(f"f_{k}{j}") for j in range(G)] for k in ("x_in", "r_in", "o_out"))
        w_in = [sem("f_w_in0"), sem("f_w_in1")]
        (chain, carrier, whi, wlo, var_ready, std_ready, y_ready, yT_psum, yhi, ylo, gu, sig, prod, hhi, hlo, d_ready,
         o_ready) = (sem("f_" + k) for k in (
             "chain", "carrier", "whi", "wlo", "var_ready", "std_ready", "y_ready", "yT_psum", "yhi", "ylo", "gu",
             "sig", "prod", "hhi", "hlo", "d_ready", "o_ready"))

        with ExitStack() as ld:
            raw = sb_in(ld)("w_raw", [P, 2, FF])
            pieces = [(w, q) for w in range(3) for q in range(KT)]

            def piece(t, q):
                return t[:].rearrange("p a b -> p (a b)")[:, q * FF:(q + 1) * FF]

            block = ld.enter_context(nc.Block())

            @block.sync
            def _(sp):
                for n, (w, q) in enumerate(pieces):
                    if n >= 2:
                        sp.wait_ge(wlo, n - 1)
                    sp.dma_start(raw[:, n % 2, :], wT_d[w].rearrange("p a b -> p (a b)")[:, q * FF:(q + 1) * FF]
                                 ).then_inc(w_in[n % 2], 16)

            @block.scalar
            def _(act):
                for n, (w, q) in enumerate(pieces):
                    act.wait_ge(w_in[n % 2], 16 * (n // 2 + 1))
                    nc.scalar.copy(piece(wT[w][0], q), raw[:, n % 2, :]).then_inc(whi, 1)

            @block.vector
            def _(dve):
                for yp in yT:
                    nc.vector.memset(yp[:].bitcast(F32), 0.0)
                for n, (w, q) in enumerate(pieces):
                    dve.wait_ge(whi, n + 1)
                    nc.vector.tensor_tensor(piece(wT[w][1], q), raw[:, n % 2, :], piece(wT[w][0], q).bitcast(F32),
                                            ALU.subtract).then_inc(wlo, 1)

        block = ph.enter_context(nc.Block())

        def over_groups(eng, head, body):
            head(0, G)
            with eng.Fori(0, NG - 1) as g:
                body(g, G, C, lambda: head(g + 1, G))
            body(NG - 1, G, C, lambda: head(NG, NT - NG * G))
            body(NG, NT - NG * G, T + T % 2, lambda: None)

        @block.sync
        def _(sp):
            def load(g, tiles):
                for j in range(tiles):
                    sp.wait_ge(yT_psum, g * G + j + 1)
                    sp.dma_start(xt[0:T, j, :], x3_d[rows(g * G + j), :]).then_inc(x_in[j], 16)

            def group(g, tiles, cols, head):
                head()
                for j in range(tiles):
                    sp.wait_ge(o_out[j], 16 * g + 16)
                    sp.dma_start(xr[0:T, j, :], x3_d[rows(g * G + j), :]).then_inc(r_in[j], 16)
                for j in range(tiles):
                    sp.wait_ge(o_ready, g * G + j + G + 1)
                    sp.dma_start(out[rows(g * G + j), :], xr[0:T, j, :]).then_inc(o_out[j], 16)

            for j in range(G):
                sp.sem_inc(o_out[j], 16)
            over_groups(sp, load, group)
            for j in range(G):
                sp.wait_ge(o_out[j], 16 * (NG + (2 if j < NT - NG * G else 1)))

        @block.vector
        def _(dve):
            c = Chain(dve, chain, 3)

            def normalize(g, tiles):
                for j in range(tiles):
                    i = g * G + j
                    c.start(i)
                    dve.wait_ge(x_in[j], 16 * g + 16)
                    c.link(nc.vector.bn_stats(stats[0:T, j, :], xt[0:T, j, :]))
                    dve.sem_inc(carrier, 1)
                    nc.vector.bn_aggr(mv[0:T, j, :], stats[0:T, j, :]).then_inc(var_ready, 1)
                    dve.wait_ge(std_ready, i + 1)
                    c.link(nc.vector.reciprocal(std[0:T, j:j + 1], std[0:T, j:j + 1]))
                    c.link(nc.vector.tensor_scalar(xt[0:T, j, :], xt[0:T, j, :], mv[0:T, j, 0:1],
                                                   std[0:T, j:j + 1], ALU.subtract, ALU.mult))
                    dve.sem_inc(y_ready, 1)
                    c.end()
                for j in range(tiles):
                    i = g * G + j
                    dve.wait_ge(yhi, i + 1)
                    nc.vector.tensor_tensor(
                        yT[1][:, :, j * T:(j + 1) * T], psT[:, 0:KT * T].rearrange("p (k t) -> p k t", k=KT),
                        yT[0][:, :, j * T:(j + 1) * T].bitcast(F32), ALU.subtract).then_inc(ylo, 1)

            def group(g, tiles, cols, head):
                def low(f):
                    n, s = g * FT + f, f % 2
                    dve.wait_ge(hhi, n + 1)
                    nc.vector.tensor_tensor(hT[1][:, f, 0:cols], hid[:, s, 0:cols],
                                            hT[0][:, f, 0:cols].bitcast(F32), ALU.subtract).then_inc(hlo, 1)

                for f in range(FT):
                    n, s = g * FT + f, f % 2
                    dve.wait_ge(sig, n + 1)
                    dve.wait_ge(hlo, n + 1)
                    nc.vector.tensor_tensor(hid[:, s, 0:cols], sg[:, s, 0:cols], psU[:, s, 0:cols],
                                            ALU.mult).then_inc(prod, 1)
                    if f:
                        low(f - 1)
                low(FT - 1)
                head()
                for j in range(tiles):
                    dve.wait_ge(d_ready, g * G + j + 1)
                    dve.wait_ge(r_in[j], 16 * g + 16)
                    nc.vector.tensor_tensor(xr[0:T, j, :], psD[0:T, j, :], xr[0:T, j, :], ALU.add).then_inc(o_ready, 1)

            dve.sem_inc(o_ready, G)
            dve.sem_inc(prod, 2)
            dve.sem_inc(hlo, 2)
            over_groups(dve, normalize, group)

        @block.scalar
        def _(act):
            def high_y(g, tiles):
                for j in range(tiles):
                    i = g * G + j
                    act.wait_ge(var_ready, i + 1)
                    nc.scalar.activation(std[0:T, j:j + 1], mv[0:T, j, 1:2], ACT.Sqrt,
                                         bias=eps[0:T, :]).then_inc(std_ready, 1)
                for j in range(tiles):
                    act.wait_ge(yT_psum, g * G + j + G + 1)
                    nc.scalar.copy(yT[0][:, :, j * T:(j + 1) * T],
                                   psT[:, 0:KT * T].rearrange("p (k t) -> p k t", k=KT)).then_inc(yhi, 1)

            def group(g, tiles, cols, head):
                def high(f):
                    act.wait_ge(prod, g * FT + f + 3)
                    nc.scalar.copy(hT[0][:, f, 0:cols], hid[:, f % 2, 0:cols]).then_inc(hhi, 1)

                for f in range(FT):
                    n, s = g * FT + f, f % 2
                    act.wait_ge(gu, n + 1)
                    act.wait_ge(prod, n + 1)
                    nc.scalar.activation(sg[:, s, 0:cols], psG[:, s, 0:cols], ACT.Silu).then_inc(sig, 1)
                    if f:
                        high(f - 1)
                high(FT - 1)
                head()

            over_groups(act, high_y, group)

        @block.tensor
        def _(pe):
            pe.sem_inc(yT_psum, G)

            def transposes(g, tiles):
                for j in range(tiles):
                    i = g * G + j
                    pe.wait_ge(y_ready, i + 1)
                    if not isinstance(i, int) or i:
                        pe.wait_ge(ylo, i)
                    for k in range(KT):
                        t = nc.tensor.transpose(psT[:, k * T:(k + 1) * T], xt[0:T, j, k * P:(k + 1) * P],
                                                ident[0:T, 0:T])
                    t.then_inc(yT_psum, 1)

            def group(g, tiles, cols, head):
                pe.wait_ge(ylo, g * G + tiles)
                for f in range(FT):
                    n, s = g * FT + f, f % 2
                    pe.wait_ge(prod, n + 1)
                    for ps, w in ((psG, wT[0]), (psU, wT[1])):
                        for k in range(KT):
                            t = product3(nc, ps[:, s, 0:cols], [p[:, k, f * P:(f + 1) * P] for p in w],
                                         [p[:, k, 0:cols] for p in yT], k == 0, k == KT - 1)
                    t.then_inc(gu, 1)
                head()
                pe.wait_ge(hlo, g * FT + FT + 2)
                for j in range(tiles):
                    pe.wait_ge(o_ready, g * G + j + 1)
                    for f in range(FT):
                        t = product3(nc, psD[0:T, j, :], [p[:, f, j * T:(j + 1) * T] for p in hT],
                                     [p[:, f, :] for p in wT[2]], f == 0, f == FT - 1)
                    t.then_inc(d_ready, 1)

            over_groups(pe, transposes, group)


_INS = ['x', 'src', 'dst', 'L0_gnn_Wk', 'L0_gnn_bk', 'L0_gnn_Wq', 'L0_gnn_bq', 'L0_gnn_Wv', 'L0_gnn_bv',
        'L0_gnn_Wff', 'L0_gnn_bff', 'L0_ffn_Wa', 'L0_ffn_ba', 'L0_ffn_Ws', 'L0_ffn_bs', 'L1_gnn_W1', 'L1_gnn_b1',
        'L1_gnn_W2', 'L1_gnn_b2', 'L1_gnn_W3', 'L1_gnn_b3', 'L1_ffn_w_gate', 'L1_ffn_w_up', 'L1_ffn_w_down']


def kernel(**inputs):
    import concourse.bacc as bacc
    from concourse.bass_utils import run_bass_kernel_spmd

    nc = bacc.Bacc("TRN2", target_bir_lowering=False, num_devices=1)
    arrays, args = {}, []
    for name in _INS:
        a = np.ascontiguousarray(inputs[name])
        arrays[f"in_{name}"] = a
        args.append(nc.dram_tensor(f"in_{name}", a.shape, mybir.dt.from_np(a.dtype), kind="ExternalInput").ap())
    out = nc.dram_tensor("out", (N, D), F32, kind="ExternalOutput").ap()
    build(nc, *args, out)
    r = run_bass_kernel_spmd(nc, [arrays], core_ids=[0])
    return r.results[0]["out"]
```

```python
from contextlib import ExitStack, contextmanager

import numpy as np

import concourse.bass as bass
from concourse import mybir

F32 = mybir.dt.float32
I32 = mybir.dt.int32
U32 = mybir.dt.uint32
F32R = mybir.dt.float32r
ALU = mybir.AluOpType
ACT = mybir.ActivationFunctionType
AX = mybir.AxisListType

P = 128
N, D = 3125, 512
T = 125
NT = N // T
KT = D // P
H, DH = 8, 64
E = 53125
EC = E // T
STEP = 256
U = 8
RING = 4
NS = -(-((E + NT * (STEP - 1)) // STEP) // U) * U
SC = NS * STEP // P
STAGE = 2
AHEAD = 2 * RING
SCAT = 25
AW = D + H + 1
GE = 160
FF = 1408
FT = FF // P
EPS = 1e-5
RNE = 12582912.0


def rows(i):
    return bass.ds(i * T, T)


def over(eng, count, *stages, peel=0):
    most = max(lag for lag, _ in stages)
    first = most + most % 2
    last = first + (count - peel - first) // 2 * 2

    def items(n, parity):
        for lag, f in stages:
            if not isinstance(n, int) or 0 <= n - lag < count:
                f(n - lag, (parity - lag) % 2)

    for n in range(first):
        items(n, n % 2)
    with eng.Fori(first, last - 1, 2) as n:
        items(n, 0)
        items(n + 1, 1)
    for n in range(last, count + most):
        items(n, n % 2)


def lap(i, s):
    return 8 * i + (16 - 8 * s)


@contextmanager
def phase(nc, dmas=(), reached=0):
    with ExitStack() as stack:
        used = []

        def sem(name):
            used.append(stack.enter_context(nc.semaphore(name)))
            return used[-1]

        yield sem
        with nc.Block() as block:
            @block.sync
            def _(sp):
                for s in used:
                    sp.sem_clear(s)

            if dmas:
                @block.gpsimd
                def _(pool):
                    for s in dmas:
                        pool.wait_ge(s, reached)
                    pool.dma_reset()
                    for s in dmas:
                        pool.sem_clear(s)


class Chain:

    def __init__(self, eng, sem, per=0):
        self.eng, self.sem, self.per, self.base, self.n = eng, sem, per, 0, 0

    def start(self, i):
        self.base, self.n = i * self.per, 0

    def link(self, ins):
        self.n += 1
        ins.then_inc(self.sem, 1)
        self.eng.wait_ge(self.sem, self.base + self.n)

    def end(self):
        assert self.n == self.per, (self.n, self.per)


def build(nc, x, src, dst, Wk, bk, Wq, bq, Wv, bv, Wff, bff, Wa, ba, Ws, bs,
          W1, b1, W2, b2, W3, b3, w_gate, w_up, w_down, out):
    dram = lambda name, shape, dt=F32: nc.dram_tensor(name, shape, dt, kind="Internal").ap()
    slots_d = dram("slots_d", [P * SC, 2], I32)
    k_d, v_d = dram("k_d", [N, D]), dram("v_d", [N, D])
    g_d = [dram("g0_d", [N, D]), dram("g1_d", [N, D])]
    wT_d = [dram("wgT_d", [P, KT, FF]), dram("wuT_d", [P, KT, FF]), dram("wdT_d", [P, FT, D])]

    with ExitStack() as whole:
        def sb_in(stack):
            return lambda name, shape, dt=F32: stack.enter_context(nc.sbuf_tensor(name, shape, dt))

        sb = sb_in(whole)

        landed = [whole.enter_context(nc.semaphore(f"landed{r}")) for r in range(RING)]
        ident = sb("ident", [P, P])
        eps = sb("eps", [P, 1])
        graph = ExitStack()
        gb = sb_in(graph)
        iota_t = gb("iota_t", [P, T])
        slot_src = gb("slot_src", [P, SC + AHEAD], U32)
        slot_dst = gb("slot_dst", [P, SC + AHEAD])
        step_tile = gb("step_tile", [1, NS], I32)
        e9 = gb("e9", [P, SC * (H + 1)])
        dis = gb("dis", [P, NT])
        acc = gb("acc", [P, NT * AW])
        nibble_w = nibble_weights(gb)

        deal = ExitStack()
        addr = sb_in(deal)("addr", [P, EC], U32)
        pair = sb_in(deal)("pair", [P, EC, 2], I32)
        place_edges(nc, sb_in, dict(ident=ident, eps=eps, iota_t=iota_t, slot_src=slot_src, slot_dst=slot_dst,
                                    step_tile=step_tile, e9=e9, x_sb=acc, addr=addr, pair=pair), x, src, dst, slots_d,
                    nibble_w, Wa, ba, Ws, bs)
        project(nc, sb_in, ident, eps, acc, Wq, bq, Wk, bk, Wv, bv, k_d, v_d,
                addr, pair, slots_d, slot_src, slot_dst, w_gate, w_up, w_down, wT_d,
                landed[0])
        deal.close()
        score_pass(nc, sb_in, ident, iota_t, slot_src, slot_dst, step_tile, e9, acc, k_d, landed)
        softmax_weights(nc, sb_in, slot_dst, e9, acc)
        aggregate(nc, sb_in, "att", iota_t, slot_src, slot_dst, step_tile, v_d, acc, e9, landed)
        gcn = ExitStack()
        x2 = sb_in(gcn)("x2", [P, NT * D])
        after_attention(nc, sb_in, ident, eps, x, Wff, bff, nibble_w, acc, dis, x2, g_d[0])
        for n, (W, b) in enumerate(((W1, b1), (W2, b2), (W3, b3))):
            aggregate(nc, sb_in, f"gcn{n}", iota_t, slot_src, slot_dst, step_tile, g_d[n % 2], acc, None,
                      landed)
            gcn_dense(nc, sb_in, n, ident, W, b, acc, dis, x2, g_d[(n + 1) % 2])
        gcn.close()
        graph.close()
        swiglu(nc, sb_in, ident, eps, wT_d, g_d[1], out)


def place_edges(nc, sb_in, c, x, src, dst, slots_d, nibble_w, Wa, ba, Ws, bs):
    ident, iota_t, slot_dst, step_tile, e9 = c["ident"], c["iota_t"], c["slot_dst"], c["step_tile"], c["e9"]
    x_sb, addr, pay = c["x_sb"], c["addr"], c["pair"]
    with phase(nc) as sem, ExitStack() as ph:
        sb = sb_in(ph)
        iota_i = sb("iota_i", [P, T], I32)
        tri = sb("tri", [P, P])
        ones = sb("ones", [P, P])
        slot0_i = sb("slot0_i", [1, NS], I32)
        slot0 = sb("slot0", [1, NS])
        tile_f = sb("tile_f", [1, NS])
        blank = sb("blank", [P, SC, 2], I32)
        edges = sb("edges", [P, 2, EC], I32)
        dst_f = sb("dst_f", [P, EC])
        tile_of = sb("tile_of", [P, EC])
        local = sb("local", [P, EC])
        member = sb("member", [P, NT * EC])
        prefix = sb("prefix", [P, NT * EC])
        cnt = sb("cnt", [P, NT])
        base = sb("base", [P, NT])
        size_i = sb("size_i", [P, NT], I32)
        size = sb("size", [P, NT])
        end = sb("end", [P, NT])
        adj = sb("adj", [P, NT])
        pos = sb("pos", [P, EC])
        pos_i = sb("pos_i", [P, EC], I32)
        part_i = sb("part_i", [P, EC], I32)
        part = sb("part", [P, EC])
        pcount = ph.enter_context(nc.psum_tensor("pcount", [P, 2, 512], F32))
        pw = ph.enter_context(nc.psum_tensor("pw", [P, 2, 2, 512], F32))
        nibble_in, w2_turned = sem("nibble_in"), sem("w2_turned")
        nibble_loads = 16 * 2 * (5 + 6 + 1)

        edges_in, pool_consts, blank_ready = sem("edges_in"), sem("pool_consts"), sem("blank_ready")
        blank_out, chain, cnt_ready, counted = sem("blank_out"), sem("deal_chain"), sem("cnt_ready"), sem("counted")
        tri0, id0, x_loaded = sem("tri0"), sem("id0"), sem("x_loaded")
        block = ph.enter_context(nc.Block())

        @block.sync
        def _(sp):
            sp.dma_start(edges[0:T, 0, :], src.rearrange("(p c) -> p c", p=T)).then_inc(edges_in, 16)
            sp.dma_start(edges[0:T, 1, :], dst.rearrange("(p c) -> p c", p=T)).then_inc(edges_in, 16)
            for t in range(0, NT, 5):
                sp.dma_start(x_sb[0:T, t * D:(t + 5) * D].rearrange("p (t d) -> p t d", d=D),
                             x[t * T:(t + 5) * T, :].rearrange("(t p) d -> p t d", p=T)).then_inc(x_loaded, 16)
            load_nibble_weights(nc, sp, nibble_w, nibble_in, Wa, ba, Ws, bs)
            sp.wait_ge(blank_ready, 2)
            sp.dma_start(slots_d.rearrange("(p c) two -> p c two", p=P), blank[:]).then_inc(blank_out, 16)
            sp.wait_ge(blank_out, 16)
            sp.wait_ge(x_loaded, 16 * (NT // 5))

        @block.gpsimd
        def _(pool):
            nc.gpsimd.iota(iota_i[:], [[1, T]], base=0, channel_multiplier=0).then_inc(pool_consts, 1)
            nc.gpsimd.iota(slot0_i[:], [[STEP, NS]], base=0, channel_multiplier=0).then_inc(pool_consts, 1)
            nc.gpsimd.memset(tri[:], 1.0).then_inc(tri0, 1)
            nc.gpsimd.memset(ident[:], 0.0).then_inc(id0, 1)
            pool.wait_ge(tri0, 1)
            nc.gpsimd.affine_select(out=tri[:], in_=tri[:], compare_op=ALU.is_gt, fill=0.0, base=0,
                                    pattern=[[1, P]], channel_multiplier=-1).then_inc(pool_consts, 1)
            pool.wait_ge(id0, 1)
            nc.gpsimd.affine_select(out=ident[:], in_=ident[:], compare_op=ALU.not_equal, fill=1.0, base=0,
                                    pattern=[[1, P]], channel_multiplier=-1).then_inc(pool_consts, 1)

        @block.tensor
        def _(pe):
            pe.wait_ge(pool_consts, 4)
            pe.wait_ge(nibble_in, nibble_loads)
            for q in range(2):
                for n, o, m in GE_PARTS:
                    for n2, o2, m2 in GE_PARTS:
                        t = nc.tensor.transpose(pw[0:m, q, n, o2:o2 + m2], nibble_w["w2n"][0:m2, q, n2, o:o + m],
                                                ident[0:m2, 0:m2])
            t.then_inc(w2_turned, 1)
            pe.wait_ge(cnt_ready, 2)
            nc.tensor.matmul(pcount[0:T, 0, 0:NT], tri[0:T, 0:T], cnt[0:T, :], start=True, stop=True)
            nc.tensor.matmul(pcount[0:T, 1, 0:NT], ones[0:T, 0:T], cnt[0:T, :],
                             start=True, stop=True).then_inc(counted, 1)

        @block.vector
        def _(dve):
            done = [0]

            def link(ins):
                done[0] += 1
                ins.then_inc(chain, 1)
                dve.wait_ge(chain, done[0])

            nc.vector.memset(blank[:, :, 0:1], 0).then_inc(blank_ready, 1)
            nc.vector.memset(blank[:, :, 1:2], -1).then_inc(blank_ready, 1)
            nc.vector.memset(ones[:], 1.0).then_inc(cnt_ready, 1)
            nc.vector.memset(c["eps"][:], EPS)
            nc.vector.memset(e9[:], 1.0)
            nc.vector.memset(slot_dst[:, SC:SC + AHEAD], -1.0)
            nc.vector.memset(c["slot_src"][:, SC:SC + AHEAD], 0)
            dve.wait_ge(edges_in, 32)
            nc.vector.tensor_copy(pay[0:T, :, 0:1], edges[0:T, 0, :].rearrange("p (c o) -> p c o", o=1))
            link(nc.vector.tensor_copy(dst_f[0:T, :], edges[0:T, 1, :]))
            link(nc.vector.tensor_scalar(tile_of[0:T, :], dst_f[0:T, :], float(T), None, ALU.is_ge))
            for t in range(2, NT):
                link(nc.vector.scalar_tensor_tensor(out=tile_of[0:T, :], in0=dst_f[0:T, :], scalar=float(t * T),
                                                    in1=tile_of[0:T, :], op0=ALU.is_ge, op1=ALU.add))
            link(nc.vector.scalar_tensor_tensor(out=local[0:T, :], in0=tile_of[0:T, :], scalar=-float(T),
                                                in1=dst_f[0:T, :], op0=ALU.mult, op1=ALU.add))
            nc.vector.tensor_copy(pay[0:T, :, 1:2], local[0:T, :].rearrange("p (c o) -> p c o", o=1))
            for t in range(NT):
                m = nc.vector.tensor_scalar(member[0:T, t * EC:(t + 1) * EC], tile_of[0:T, :], float(t), None,
                                            ALU.is_equal)
            link(m)
            link(nc.vector.tensor_tensor_scan(prefix[0:T, :], ones[0:T, 0:1].to_broadcast([T, NT * EC]),
                                              member[0:T, :], 0.0, ALU.mult, ALU.add))
            pre = prefix[0:T, :].rearrange("p (t c) -> p t c", t=NT)
            nc.vector.memset(base[0:T, 0:1], 0.0)
            link(nc.vector.tensor_copy(base[0:T, 1:NT], pre[:, 0:NT - 1, EC - 1]))
            nc.vector.tensor_tensor(cnt[0:T, :], pre[:, :, EC - 1], base[0:T, :],
                                    ALU.subtract).then_inc(cnt_ready, 1)
            dve.wait_ge(w2_turned, 1)
            for q in range(2):
                for n, o, m in GE_PARTS:
                    nc.vector.tensor_copy(nibble_w["w2"][0:m, q, n, :], pw[0:m, q, n, 0:GE])
            dve.wait_ge(counted, 1)
            link(nc.vector.tensor_scalar(size_i[0:T, :], pcount[0:T, 1, 0:NT], float(STEP - 1), None, ALU.add))
            link(nc.vector.tensor_scalar(size_i[0:T, :], size_i[0:T, :], -STEP, None, ALU.bitwise_and))
            link(nc.vector.tensor_copy(size[0:T, :], size_i[0:T, :]))
            link(nc.vector.tensor_tensor_scan(end[0:T, :], ones[0:T, 0:NT], size[0:T, :], 0.0, ALU.mult, ALU.add))
            link(nc.vector.tensor_tensor(adj[0:T, :], end[0:T, :], size[0:T, :], ALU.subtract))
            link(nc.vector.tensor_tensor(adj[0:T, :], adj[0:T, :], base[0:T, :], ALU.subtract))
            link(nc.vector.scalar_tensor_tensor(out=adj[0:T, :], in0=pcount[0:T, 0, 0:NT], scalar=-1.0,
                                                in1=adj[0:T, :], op0=ALU.add, op1=ALU.add))
            for t in range(NT):
                s = slice(t * EC, (t + 1) * EC)
                m = nc.vector.scalar_tensor_tensor(out=prefix[0:T, s], in0=prefix[0:T, s], scalar=adj[0:T, t:t + 1],
                                                   in1=member[0:T, s], op0=ALU.add, op1=ALU.mult)
            link(m)
            link(nc.vector.tensor_reduce(pos[0:T, :], prefix[0:T, :].rearrange("p (t c) -> p c t", t=NT),
                                         AX.X, ALU.add))
            link(nc.vector.tensor_copy(pos_i[0:T, :], pos[0:T, :]))
            link(nc.vector.tensor_scalar(part_i[0:T, :], pos_i[0:T, :], P - 1, None, ALU.bitwise_and))
            link(nc.vector.tensor_scalar(pos_i[0:T, :], pos_i[0:T, :], 7, None, ALU.arith_shift_right))
            link(nc.vector.tensor_copy(part[0:T, :], part_i[0:T, :]))
            link(nc.vector.tensor_copy(pos[0:T, :], pos_i[0:T, :]))
            link(nc.vector.scalar_tensor_tensor(out=pos[0:T, :], in0=part[0:T, :], scalar=float(SC),
                                                in1=pos[0:T, :], op0=ALU.mult, op1=ALU.add))
            nc.vector.tensor_copy(addr[0:T, :], pos[0:T, :])
            dve.wait_ge(pool_consts, 4)
            nc.vector.tensor_copy(iota_t[:], iota_i[:])
            link(nc.vector.tensor_copy(slot0[:], slot0_i[:]))
            link(nc.vector.tensor_scalar(tile_f[:], slot0[:], end[0:1, 0:1], None, ALU.is_ge))
            for t in range(1, NT - 1):
                link(nc.vector.scalar_tensor_tensor(out=tile_f[:], in0=slot0[:], scalar=end[0:1, t:t + 1],
                                                    in1=tile_f[:], op0=ALU.is_ge, op1=ALU.add))
            nc.vector.tensor_copy(step_tile[:], tile_f[:])


def project(nc, sb_in, ident, eps, xq, Wq, bq, Wk, bk, Wv, bv, k_d, v_d,
            addr, pair, slots_d, slot_src, slot_dst, w_gate, w_up, w_down, wT_d,
            scattered):
    with phase(nc, [scattered], 16 * EC) as sem, ExitStack() as ph:
        sb = sb_in(ph)
        w_hi = sb("w_qkv_hi", [P, 3, KT, D], F32R)
        w_lo = sb("w_qkv_lo", [P, 3, KT, D], F32R)
        w = sb("w_qkv", [P, 3, KT, D])
        b = sb("b_qkv", [P, 3, D])
        stage_addr = sb("stage_addr", [P, SCAT], U32)
        stage_pair = sb("stage_pair", [P, SCAT, 2], I32)
        back = sb("back", [P, SC, 2], I32)
        stats = sb("stats", [P, 2, 6])
        mv = sb("mv", [P, 2, 2])
        std = sb("std", [P, 2, 1])
        rstd = sb("rstd", [P, 2, 1])
        y = sb("y", [P, 2, D])
        yT_hi = sb("yT_hi1", [P, 2, KT * T], F32R)
        yT_lo = sb("yT_lo1", [P, 2, KT * T], F32R)
        kv = sb("kv", [P, 2, 2, D])
        psT = ph.enter_context(nc.psum_tensor("psT1", [P, 2, 512], F32))
        psM = ph.enter_context(nc.psum_tensor("psM1", [P, 3, 512], F32))
        w_in = [sem(f"wqkv_in{n}") for n in range(3)]
        b_in, chain, carrier = sem("bqkv_in"), sem("p1_chain"), sem("p1_carrier")
        staged, turn, baclanded = sem("staged"), sem("deal_turn"), sem("baclanded")
        whi_ready, wlo_ready, var_ready, std_ready, y_ready, yT_psum, hi_ready, lo_ready, m_ready, added = (
            sem("p1_" + n) for n in ("whi_ready", "wlo_ready", "var_ready", "std_ready", "y_ready", "yT_psum",
                                     "hi_ready", "lo_ready", "m_ready", "added"))
        kv_out = [sem("p1_kv_out0"), sem("p1_kv_out1")]
        ternary = Ternary(nc, sem, sb, ph, ident, w_gate, w_up, w_down, wT_d)
        block = ph.enter_context(nc.Block())

        @block.sync
        def _(sp):
            for n, W in enumerate((Wq, Wk, Wv)):
                sp.dma_start(w[:, n], W.rearrange("(k p) n -> p k n", p=P)).then_inc(w_in[n], 16)
            for n, v in enumerate((bq, bk, bv)):
                sp.dma_start(b[:, n, :], v.rearrange("(o n) -> o n", o=1).to_broadcast([P, D])).then_inc(b_in, 16)

            def store(i, s):
                sp.wait_ge(added, 3 * i + 6)
                sp.dma_start(k_d[rows(i), :], kv[0:T, s, 0, :]).then_inc(kv_out[s], 16)
                sp.dma_start(v_d[rows(i), :], kv[0:T, s, 1, :]).then_inc(kv_out[s], 16)

            over(sp, NT, (0, store))
            ternary.loads_and_stores(sp)
            sp.wait_ge(kv_out[0], 32 * (NT // 2 + 2))
            sp.wait_ge(kv_out[1], 32 * (NT // 2 + 1))
            sp.wait_ge(scattered, 16 * EC)
            sp.dma_start(back[:], slots_d.rearrange("(p c) two -> p c two", p=P)).then_inc(baclanded, 16)

        @block.gpsimd
        def _(pool):
            def scatter(i):
                nc.gpsimd.tensor_copy(stage_addr[0:T, :], addr[0:T, bass.ds(i * SCAT, SCAT)]).then_inc(staged, 1)
                nc.gpsimd.tensor_copy(stage_pair[0:T], pair[0:T, bass.ds(i * SCAT, SCAT), :]).then_inc(staged, 1)
                pool.wait_ge(staged, 2 * i + 2)
                pool.sem_inc(turn, 1)
                for j in range(SCAT):
                    nc.gpsimd.indirect_dma_start(
                        slots_d, bass.IndirectOffsetOnAxis(ap=stage_addr[0:T, j:j + 1], axis=0),
                        stage_pair[0:T, j, :], None).then_inc(scattered, 16)

            scatter(0)
            with pool.Fori(1, EC // SCAT) as i:
                pool.wait_ge(scattered, 16 * SCAT * i)
                pool.sem_inc(turn, 1)
                scatter(i)

        @block.vector
        def _(dve):
            dve.sem_inc(y_ready, 2)
            dve.sem_inc(lo_ready, 2)
            dve.sem_inc(added, 3)
            dve.sem_inc(kv_out[0], 32)
            dve.sem_inc(kv_out[1], 32)
            for n in range(3):
                dve.wait_ge(whi_ready, n + 1)
                nc.vector.tensor_tensor(w_lo[:, n], w[:, n], w_hi[:, n].bitcast(F32),
                                        ALU.subtract).then_inc(wlo_ready, 1)
            dve.wait_ge(b_in, 48)
            c = Chain(dve, chain, 2)

            def normalize(i, s):
                c.start(i)
                xt = xq[0:T, bass.ds(i * D, D)]
                c.link(nc.vector.bn_stats(stats[0:T, s, :], xt))
                dve.sem_inc(carrier, 1)
                nc.vector.bn_aggr(mv[0:T, s, :], stats[0:T, s, :]).then_inc(var_ready, 1)
                dve.wait_ge(std_ready, i + 1)
                c.link(nc.vector.reciprocal(rstd[0:T, s, :], std[0:T, s, :]))
                dve.wait_ge(yT_psum, i + 1)
                nc.vector.tensor_scalar(y[0:T, s, :], xt, mv[0:T, s, 0:1], rstd[0:T, s, 0:1],
                                        ALU.subtract, ALU.mult).then_inc(y_ready, 1)
                c.end()

            def low(i, s):
                dve.wait_ge(hi_ready, i + 1)
                nc.vector.tensor_tensor(yT_lo[:, s, :], psT[:, s, 0:KT * T], yT_hi[:, s, :].bitcast(F32),
                                        ALU.subtract).then_inc(lo_ready, 1)

            def add_biases(i, s):
                dve.wait_ge(m_ready, 3 * i + 7)
                nc.vector.tensor_tensor(xq[0:T, bass.ds(i * D, D)], psM[0:T, 0, :], b[0:T, 0, :],
                                        ALU.add).then_inc(added, 1)
                dve.wait_ge(kv_out[s], 2 * lap(i, s))
                for n in (1, 2):
                    dve.wait_ge(m_ready, 3 * i + 7 + n)
                    nc.vector.tensor_tensor(kv[0:T, s, n - 1], psM[0:T, n, :], b[0:T, n, :],
                                            ALU.add).then_inc(added, 1)

            over(dve, NT, (0, normalize), (1, low), (2, add_biases))
            ternary.quantize(dve)
            dve.wait_ge(baclanded, 16)
            nc.vector.tensor_copy(slot_src[:, 0:SC].rearrange("p (c o) -> p c o", o=1), back[:, :, 0:1])
            nc.vector.tensor_copy(slot_dst[:, 0:SC].rearrange("p (c o) -> p c o", o=1), back[:, :, 1:2])

        @block.scalar
        def _(act):
            def root(i, s):
                act.wait_ge(var_ready, i + 1)
                nc.scalar.activation(std[0:T, s, :], mv[0:T, s, 1:2], ACT.Sqrt,
                                     bias=eps[0:T, :]).then_inc(std_ready, 1)

            def turn(i, s):
                act.wait_ge(yT_psum, i + 3)
                act.wait_ge(m_ready, 3 * i + 3)
                nc.scalar.copy(yT_hi[:, s, :], psT[:, s, 0:KT * T]).then_inc(hi_ready, 1)

            for n in range(3):
                act.wait_ge(w_in[n], 16)
                nc.scalar.copy(w_hi[:, n], w[:, n]).then_inc(whi_ready, 1)
            over(act, NT, (0, root), (1, turn))
            ternary.place(act)

        @block.tensor
        def _(pe):
            pe.sem_inc(yT_psum, 2)
            pe.sem_inc(m_ready, 6)

            def transposes(i, s):
                pe.wait_ge(y_ready, i + 3)
                pe.wait_ge(lo_ready, i + 1)
                for k in range(KT):
                    t = nc.tensor.transpose(psT[:, s, k * T:(k + 1) * T], y[0:T, s, k * P:(k + 1) * P],
                                            ident[0:T, 0:T])
                t.then_inc(yT_psum, 1)

            def products(i, s):
                if isinstance(i, int) and i == 0:
                    pe.wait_ge(wlo_ready, 3)
                pe.wait_ge(lo_ready, i + 3)
                for n in range(3):
                    pe.wait_ge(added, 3 * i + n + 1)
                    for k in range(KT):
                        c = slice(k * T, (k + 1) * T)
                        t = product3(nc, psM[0:T, n, :], (yT_hi[:, s, c], yT_lo[:, s, c]),
                                     (w_hi[:, n, k, :], w_lo[:, n, k, :]), k == 0, k == KT - 1)
                    t.then_inc(m_ready, 1)

            over(pe, NT, (0, transposes), (1, products))
            ternary.transpose(pe)


def chunk_pair(t, s, width):
    return t[:, bass.ds(s * 2 * width, 2 * width)].rearrange("p (c w) -> p c w", c=2)


def distances(nc, off, iota_t, slot_dst, s, b):
    for h in range(2):
        t = nc.scalar.activation(off[:, b, h, :], iota_t[:], ACT.Abs, scale=-1.0,
                                 bias=slot_dst[:, bass.ds(s * 2 + h, 1)])
    return t


def onehots(nc, oh, off, b):
    return nc.scalar.activation(oh[:, b], off[:, b], ACT.Relu, scale=-1.0, bias=1.0)


def stage_index(nc, act, slot_src, index, i, u, consumed, index_ready):
    act.wait_ge(consumed, i + u + RING)
    nc.scalar.copy(index[:, u // RING % 2, :], slot_src[:, bass.ds((i + u) * 2, 2 * RING)]).then_inc(index_ready, 1)


def gather_steps(nc, pool, rows_d, index, index_ready, buf, consumed, turn, landed):
    with pool.Fori(0, NS - U + 1, U) as i:
        for u in range(U):
            if u % RING == 0:
                pool.wait_ge(index_ready, i // RING + u // RING + 1)
                pool.sem_inc(turn, 1)
            pool.wait_ge(consumed, i + u + RING + 1)
            pool.sem_inc(turn, 1)
            for h in range(2):
                col = 2 * (u % RING) + h
                nc.gpsimd.indirect_dma_start(
                    buf[:, u % RING, h * D:(h + 1) * D], None, rows_d,
                    bass.IndirectOffsetOnAxis(ap=index[:, u // RING, col:col + 1], axis=0)
                ).then_inc(landed[u % RING], 16)


def score_pass(nc, sb_in, ident, iota_t, slot_src, slot_dst, step_tile, e9, q_sb, k_d, landed):
    with phase(nc, landed, 32 * NS // RING) as sem, ExitStack() as ph:
        sb = sb_in(ph)
        index = sb("landeddex", [P, 2, 2 * RING], U32)
        krows = sb("krows", [P, RING, 2 * D])
        off = sb("off2", [P, 2, 2, T])
        oh = sb("oh2", [P, 2, 2, T])
        ohT = sb("ohT", [P, 2, 2 * P])
        prod = sb("prod", [P, RING, 2 * D])
        psT = ph.enter_context(nc.psum_tensor("psT2", [P, 2, 512], F32))
        psQ = ph.enter_context(nc.psum_tensor("psQ2", [P, 2, 1024], F32))
        index_ready, turn, off_ready, oh_ready, ohT_psum, ohT_ready, q_ready, scored, reduced = (
            sem("p2_" + n) for n in ("index_ready", "turn", "off_ready", "oh_ready", "ohT_psum", "ohT_ready",
                                     "q_ready", "scored", "reduced"))
        block = ph.enter_context(nc.Block())

        @block.gpsimd
        def _(pool):
            gather_steps(nc, pool, k_d, index, index_ready, krows, scored, turn, landed)

        @block.scalar
        def _(act):
            act.sem_inc(ohT_ready, 2)

            def turn_onehots(s, b):
                act.wait_ge(ohT_psum, s + 3)
                act.wait_ge(q_ready, s + 1)
                nc.scalar.copy(ohT[0:T, b, :], psT[0:T, b, 0:2 * P]).then_inc(ohT_ready, 1)

            stage_index(nc, act, slot_src, index, 0, 0, scored, index_ready)
            for b in range(2):
                distances(nc, off, iota_t, slot_dst, b, b).then_inc(off_ready, 1)
                act.wait_ge(off_ready, b + 1)
                onehots(nc, oh, off, b).then_inc(oh_ready, 1)
            turn_onehots(0, 0)
            with act.Fori(0, NS - U + 1, U) as i:
                for u in range(U):
                    if u % RING == STAGE:
                        stage_index(nc, act, slot_src, index, i, u - STAGE + RING, scored, index_ready)
                    distances(nc, off, iota_t, slot_dst, i + u + 2, u % 2).then_inc(off_ready, 1)
                    turn_onehots(i + u + 1, (u + 1) % 2)
                    act.wait_ge(off_ready, i + u + 3)
                    onehots(nc, oh, off, u % 2).then_inc(oh_ready, 1)

        @block.tensor
        def _(pe):
            pe.sem_inc(ohT_psum, 2)
            pe.sem_inc(q_ready, 2)

            def transposes(s, b):
                pe.wait_ge(oh_ready, s + 1)
                pe.wait_ge(ohT_ready, s + 1)
                for h in range(2):
                    t = nc.tensor.transpose(psT[0:T, b, h * P:(h + 1) * P], oh[:, b, h, :], ident[:])
                t.then_inc(ohT_psum, 1)

            transposes(0, 0)
            with pe.Fori(0, NS - U + 1, U) as i:
                for u in range(U):
                    s, b = i + u, u % 2
                    transposes(s + 1, (u + 1) % 2)
                    tile = pe.value_load(step_tile[0:1, bass.ds(s, 1)], min_val=0, max_val=NT - 1)
                    pe.wait_ge(ohT_ready, s + 3)
                    pe.wait_ge(scored, s + RING + 3)
                    for h in range(2):
                        t = nc.tensor.matmul(psQ[:, b, h * D:(h + 1) * D], ohT[0:T, b, h * P:(h + 1) * P],
                                             q_sb[0:T, bass.ds(tile * D, D)], start=True, stop=True)
                    t.then_inc(q_ready, 1)

        @block.vector
        def _(dve):
            dve.sem_inc(scored, 2 * RING)
            dve.sem_inc(reduced, RING)

            def multiply(i, u):
                s, r = i + u, u % RING
                dve.wait_ge(landed[r], i * (32 // RING) + 32 * (u // RING + 1))
                dve.wait_ge(q_ready, s + 3)
                dve.wait_ge(reduced, s + 1)
                nc.vector.tensor_tensor(prod[:, r, :], psQ[:, u % 2, :], krows[:, r, :], ALU.mult).then_inc(scored, 1)

            def reduce(i, u):
                s = i + u
                dve.wait_ge(scored, s + 2 * RING + 1)
                nc.vector.tensor_reduce(chunk_pair(e9, s, H + 1)[:, :, 0:H],
                                        prod[:, u % RING, :].rearrange("p (c h d) -> p c h d", c=2, h=H),
                                        AX.X, ALU.add).then_inc(reduced, 1)

            with dve.Fori(0, NS - U + 1, U) as i:
                for u in range(U):
                    multiply(i, u)
                    if u:
                        reduce(i, u - 1)
                reduce(i, U - 1)


def softmax_weights(nc, sb_in, slot_dst, e9, acc):
    with phase(nc) as sem, ExitStack() as ph:
        sb = sb_in(ph)
        empty = sb("empty", [P, SC])
        most = sb("most", [P, 1])
        top = sb("top", [P, 1])
        shift = sb("shift", [P, 1])
        chain, most_ready, top_ready, shift_ready = sem("p3_chain"), sem("most"), sem("top"), sem("shift")
        scores = e9[:].rearrange("p (c w) -> p c w", w=H + 1)[:, :, 0:H]
        block = ph.enter_context(nc.Block())

        @block.vector
        def _(dve):
            c = Chain(dve, chain)
            c.link(nc.vector.tensor_scalar(empty[:], slot_dst[:, 0:SC], 0.0, -1e30, ALU.is_lt, ALU.mult))
            c.link(nc.vector.tensor_tensor(
                scores, scores, empty[:].rearrange("p (c w) -> p c w", w=1).to_broadcast([P, SC, H]), ALU.add))
            nc.vector.tensor_reduce(most[:], scores, AX.XY, ALU.max).then_inc(most_ready, 1)
            dve.wait_ge(top_ready, 1)
            nc.vector.tensor_scalar(shift[:], top[:], -(DH ** -0.5), 3.0, ALU.mult, ALU.add).then_inc(shift_ready, 1)

        @block.gpsimd
        def _(pool):
            nc.gpsimd.memset(acc[:], 0.0)
            pool.wait_ge(most_ready, 1)
            nc.gpsimd.partition_all_reduce(top[:], most[:], P, bass.bass_isa.ReduceOp.max).then_inc(top_ready, 1)

        @block.scalar
        def _(act):
            act.wait_ge(shift_ready, 1)
            nc.scalar.activation(scores, scores, ACT.Exp, bias=shift[:], scale=DH ** -0.5)


def aggregate(nc, sb_in, name, iota_t, slot_src, slot_dst, step_tile, rows_d, acc, e9, landed):
    width = AW if e9 is not None else D
    with phase(nc, landed, 32 * NS // RING) as sem, ExitStack() as ph:
        sb = sb_in(ph)
        index = sb(name + "_index", [P, 2, 2 * RING], U32)
        got = sb(name + "_rows", [P, RING, 2 * D])
        off = sb(name + "_off", [P, 2, 2, T])
        oh = sb(name + "_oh", [P, 2, 2, T])
        msg = sb(name + "_msg", [P, RING, 2 * D]) if e9 is not None else None
        ps = ph.enter_context(nc.psum_tensor(name + "_ps", [P, 2, 1024], F32))
        index_ready, turn, off_ready, oh_ready, msg_ready, summed, added = (
            sem(f"{name}_{n}") for n in ("index_ready", "turn", "off_ready", "oh_ready", "msg_ready", "summed",
                                         "added"))
        used = summed if e9 is None else msg_ready
        block = ph.enter_context(nc.Block())

        @block.gpsimd
        def _(pool):
            gather_steps(nc, pool, rows_d, index, index_ready, got, used, turn, landed)

        @block.scalar
        def _(act):
            stage_index(nc, act, slot_src, index, 0, 0, used, index_ready)
            act.sem_inc(oh_ready, 1)
            distances(nc, off, iota_t, slot_dst, 0, 0).then_inc(off_ready, 1)
            with act.Fori(0, NS - U + 1, U) as i:
                for u in range(U):
                    if u % RING == STAGE:
                        stage_index(nc, act, slot_src, index, i, u - STAGE + RING, used, index_ready)
                    act.wait_ge(oh_ready, i + u + 1)
                    distances(nc, off, iota_t, slot_dst, i + u + 1, (u + 1) % 2).then_inc(off_ready, 1)
                    act.wait_ge(off_ready, i + u + 1)
                    act.wait_ge(summed, i + u + 2 * RING - 1)
                    onehots(nc, oh, off, u % 2).then_inc(oh_ready, 1)

        def arrived(eng, i, u):
            eng.wait_ge(landed[u % RING], i * (32 // RING) + 32 * (u // RING + 1))

        def weigh(dve, i, u):
            if e9 is not None:
                s = i + u
                arrived(dve, i, u)
                dve.wait_ge(summed, s + RING + 1)
                nc.vector.tensor_tensor(
                    msg[:, u % RING, :].rearrange("p (c h d) -> p c h d", c=2, h=H),
                    got[:, u % RING, :].rearrange("p (c h d) -> p c h d", c=2, h=H),
                    chunk_pair(e9, s, H + 1)[:, :, 0:H].rearrange("p c (h o) -> p c h o", o=1).to_broadcast(
                        [P, 2, H, DH]), ALU.mult).then_inc(msg_ready, 1)

        @block.tensor
        def _(pe):
            pe.sem_inc(summed, 2 * RING)
            with pe.Fori(0, NS - U + 1, U) as i:
                for u in range(U):
                    s, b = i + u, u % 2
                    pe.wait_ge(oh_ready, s + 2)
                    if e9 is None:
                        arrived(pe, i, u)
                    else:
                        pe.wait_ge(msg_ready, s + 2 * RING + 1)
                    pe.wait_ge(added, s + 1)
                    for h in range(2):
                        rhs = (got if e9 is None else msg)[:, u % RING, h * D:(h + 1) * D]
                        t = nc.tensor.matmul(ps[0:T, b, 0:D], oh[:, b, h, :], rhs, start=(h == 0), stop=(h == 1))
                    if e9 is not None:
                        for h in range(2):
                            t = nc.tensor.matmul(ps[0:T, b, D:AW], oh[:, b, h, :],
                                                 e9[:, bass.ds((s * 2 + h) * (H + 1), H + 1)],
                                                 start=(h == 0), stop=(h == 1))
                    t.then_inc(summed, 1)

        @block.vector
        def _(dve):
            dve.sem_inc(added, 2)

            def add(i, u):
                s, b = i + u, u % 2
                tile = dve.value_load(step_tile[0:1, bass.ds(s, 1)], min_val=0, max_val=NT - 1)
                dve.wait_ge(added, s + 2)
                dve.wait_ge(summed, s + 2 * RING + 1)
                part = acc[0:T, bass.ds(tile * AW, width)]
                nc.vector.tensor_tensor(part, part, ps[0:T, b, 0:width], ALU.add).then_inc(added, 1)

            if e9 is not None:
                dve.sem_inc(msg_ready, 2 * RING)
            weigh(dve, 0, 0)
            weigh(dve, 0, 1)
            with dve.Fori(0, NS - 2 * U + 1, U) as i:
                for u in range(U):
                    weigh(dve, i, u + 2)
                    add(i, u)
            for u in range(U):
                if u < U - 2:
                    weigh(dve, NS - U, u + 2)
                add(NS - U, u)


def after_attention(nc, sb_in, ident, eps, x, Wff, bff, nibble_w, acc, dis, x2, g_d):
    feat_stack = ExitStack()
    sb = sb_in(feat_stack)
    nib = sb("nib", [P, NT, 4])
    marks = sb("marks", [P, NT, 3])
    opc = sb("opc", [P, NT, 2])
    attention_out(nc, sb_in, ident, eps, x, Wff, bff, acc, dis, x2, nib, marks, opc)
    res = sb("res", [P, NT, 2, 2, 2])
    nibble_pipelines(nc, sb_in, ident, nibble_w, nib, opc, res)
    alu_out(nc, sb_in, eps, marks, res, acc, dis, x2, g_d)
    feat_stack.close()


def attention_out(nc, sb_in, ident, eps, x, Wff, bff, acc, dis, x2, nib, marks, opc):
    with phase(nc) as sem, ExitStack() as ph:
        sb = sb_in(ph)
        w = sb("w_ff", [P, KT, D])
        w_hi = sb("w_ff_hi", [P, KT, D], F32R)
        w_lo = sb("w_ff_lo", [P, KT, D], F32R)
        b = sb("b_ff", [P, D])
        w16 = sb("w16", [P, 4 * 16])
        w16_i = sb("w16_i", [P, 4 * 16], I32)
        xt = sb("xt4", [P, 2, D])
        none = sb("none", [P, NT, H])
        rden = sb("rden", [P, NT, H])
        att = sb("att", [P, 2, D])
        attT_hi = sb("attT_hi", [P, 2, KT * T], F32R)
        attT_lo = sb("attT_lo", [P, 2, KT * T], F32R)
        x1 = sb("x1", [P, 2, D])
        y = sb("y4", [P, 2, D])
        stats = sb("stats4", [P, 2, 6])
        mv = sb("mv4", [P, 2, 2])
        std = sb("std4", [P, 2, 1])
        rstd = sb("rstd4", [P, 2, 1])
        bits = sb("bits", [P, 2, 64])
        psT = ph.enter_context(nc.psum_tensor("psT4", [P, 2, 512], F32))
        psM = ph.enter_context(nc.psum_tensor("psM4", [P, 2, 512], F32))
        w_in, whi_ready, wlo_ready, w16_ready, chain, chain1, chain3, carrier, deg_sqrt = (
            sem("p4_" + n) for n in ("w_in", "whi_ready", "wlo_ready", "w16_ready", "chain", "chain1", "chain3",
                                     "carrier", "deg_sqrt"))
        x_in = [sem("p4_x_in0"), sem("p4_x_in1")]
        att_ready, attT_psum, hi_ready, lo_ready, m_ready, xb_ready, x1_ready, var_ready, std_ready, x2_ready = (
            sem("p4_" + n) for n in ("att_ready", "attT_psum", "hi_ready", "lo_ready", "m_ready", "xb_ready",
                                     "x1_ready", "var_ready", "std_ready", "x2_ready"))
        pool_carrier = sem("p4_pool_carrier")
        tiles = acc[0:T, :].rearrange("p (t w) -> p t w", t=NT)
        block = ph.enter_context(nc.Block())

        @block.sync
        def _(sp):
            sp.dma_start(w[:], Wff.rearrange("(k p) n -> p k n", p=P)).then_inc(w_in, 16)
            sp.dma_start(b[:], bff.rearrange("(o n) -> o n", o=1).to_broadcast([P, D])).then_inc(w_in, 16)

            def load(i, s):
                sp.wait_ge(x1_ready, i + 1)
                sp.dma_start(xt[0:T, s, :], x[rows(i), :]).then_inc(x_in[s], 16)

            over(sp, NT, (0, load))

        @block.gpsimd
        def _(pool):
            nc.gpsimd.iota(w16_i[:], [[0, 4], [-1, 16]], base=16, channel_multiplier=0).then_inc(w16_ready, 1)
            pool.sem_inc(x2_ready, 2)
            pool.wait_ge(w_in, 32)

            def add_bias(i, s):
                pool.wait_ge(x_in[s], lap(i, s))
                pool.sem_inc(pool_carrier, 1)
                nc.gpsimd.tensor_tensor(xt[0:T, s, :], xt[0:T, s, :], b[0:T, :], ALU.add).then_inc(xb_ready, 1)

            def second_residual(i, s):
                pool.wait_ge(chain3, 3 * i + 2)
                pool.sem_inc(pool_carrier, 1)
                nc.gpsimd.tensor_tensor(x2[0:T, bass.ds(i * D, D)], x1[0:T, s, :], y[0:T, s, :],
                                        ALU.add).then_inc(x2_ready, 1)

            over(pool, NT, (0, add_bias), (1, second_residual))

        @block.scalar
        def _(act):
            act.wait_ge(w_in, 32)
            nc.scalar.copy(w_hi[:], w[:]).then_inc(whi_ready, 1)
            act.wait_ge(deg_sqrt, 1)
            nc.scalar.activation(dis[0:T, :], dis[0:T, :], ACT.Sqrt).then_inc(deg_sqrt, 1)

            def high(i, s):
                act.wait_ge(attT_psum, i + 3)
                act.wait_ge(m_ready, i + 1)
                nc.scalar.copy(attT_hi[:, s, :], psT[:, s, 0:KT * T]).then_inc(hi_ready, 1)

            def root(i, s):
                act.wait_ge(var_ready, i + 1)
                nc.scalar.activation(std[0:T, s, :], mv[0:T, s, 1:2], ACT.Sqrt, bias=eps[0:T, :]).then_inc(std_ready, 1)

            over(act, NT, (0, high), (2, root))

        @block.tensor
        def _(pe):
            pe.sem_inc(attT_psum, 2)
            pe.sem_inc(m_ready, 2)

            def transposes(i, s):
                pe.wait_ge(att_ready, i + 1)
                pe.wait_ge(lo_ready, i + 1)
                for k in range(KT):
                    t = nc.tensor.transpose(psT[:, s, k * T:(k + 1) * T], att[0:T, s, k * P:(k + 1) * P],
                                            ident[0:T, 0:T])
                t.then_inc(attT_psum, 1)

            def product(i, s):
                if isinstance(i, int) and i == 0:
                    pe.wait_ge(wlo_ready, 1)
                pe.wait_ge(lo_ready, i + 3)
                pe.wait_ge(x1_ready, i + 1)
                for k in range(KT):
                    c = slice(k * T, (k + 1) * T)
                    t = product3(nc, psM[0:T, s, :], (attT_hi[:, s, c], attT_lo[:, s, c]),
                                 (w_hi[:, k, :], w_lo[:, k, :]), k == 0, k == KT - 1)
                t.then_inc(m_ready, 1)

            over(pe, NT, (0, transposes), (1, product))

        @block.vector
        def _(dve):
            dve.sem_inc(x1_ready, 2)
            dve.sem_inc(lo_ready, 2)
            c = Chain(dve, chain)
            nc.vector.tensor_scalar(dis[0:T, :], tiles[:, :, AW - 1], 1.0, None, ALU.add).then_inc(deg_sqrt, 1)
            den = tiles[:, :, D:D + H]
            c.link(nc.vector.tensor_scalar(none[0:T], den, 0.0, None, ALU.is_equal))
            c.link(nc.vector.tensor_tensor(rden[0:T], den, none[0:T], ALU.add))
            c.link(nc.vector.reciprocal(rden[0:T], rden[0:T]))
            dve.wait_ge(w16_ready, 1)
            c.link(nc.vector.tensor_copy(w16[:], w16_i[:]))
            dve.wait_ge(deg_sqrt, 2)
            c.link(nc.vector.reciprocal(dis[0:T, :], dis[0:T, :]))
            dve.wait_ge(whi_ready, 1)
            nc.vector.tensor_tensor(w_lo[:], w[:], w_hi[:].bitcast(F32), ALU.subtract).then_inc(wlo_ready, 1)
            c1, c3 = Chain(dve, chain1, 1), Chain(dve, chain3, 3)

            def divide(i, s):
                dve.wait_ge(attT_psum, i + 1)
                nc.vector.tensor_tensor(
                    att[0:T, s, :].rearrange("p (h d) -> p h d", h=H),
                    acc[0:T, bass.ds(i * AW, D)].rearrange("p (h d) -> p h d", h=H),
                    rden[0:T, bass.ds(i, 1), :].rearrange("p o h -> p h o").to_broadcast([T, H, DH]),
                    ALU.mult).then_inc(att_ready, 1)

            def low(i, s):
                dve.wait_ge(hi_ready, i + 1)
                nc.vector.tensor_tensor(attT_lo[:, s, :], psT[:, s, 0:KT * T], attT_hi[:, s, :].bitcast(F32),
                                        ALU.subtract).then_inc(lo_ready, 1)

            def residual(i, s):
                c1.start(i)
                dve.wait_ge(xb_ready, i + 1)
                dve.wait_ge(m_ready, i + 3)
                dve.wait_ge(x2_ready, i + 1)
                nc.vector.tensor_tensor(x1[0:T, s, :], psM[0:T, s, :], xt[0:T, s, :], ALU.add).then_inc(x1_ready, 1)
                dve.wait_ge(x1_ready, i + 3)
                c1.link(nc.vector.bn_stats(stats[0:T, s, :], x1[0:T, s, :]))
                dve.sem_inc(carrier, 1)
                nc.vector.bn_aggr(mv[0:T, s, :], stats[0:T, s, :]).then_inc(var_ready, 1)
                c1.end()

            def features(i, s):
                c3.start(i)
                dve.wait_ge(std_ready, i + 1)
                c3.link(nc.vector.reciprocal(rstd[0:T, s, :], std[0:T, s, :]))
                c3.link(nc.vector.tensor_scalar(y[0:T, s, :], x1[0:T, s, :], mv[0:T, s, 0:1], rstd[0:T, s, 0:1],
                                                ALU.subtract, ALU.mult))
                c3.link(nc.vector.scalar_tensor_tensor(out=bits[0:T, s, :], in0=y[0:T, s, 16:80], scalar=0.5,
                                                       in1=w16[0:T, :], op0=ALU.is_gt, op1=ALU.mult))
                nc.vector.tensor_reduce(nib[0:T, bass.ds(i, 1), :],
                                        bits[0:T, s, :].rearrange("p (f o j) -> p f o j", f=1, j=16),
                                        AX.X, ALU.max)
                nc.vector.tensor_scalar(marks[0:T, bass.ds(i, 1), :],
                                        y[0:T, s, 0:3].rearrange("p (f j) -> p f j", f=1), 0.5, None, ALU.is_gt)
                nc.vector.tensor_copy(opc[0:T, bass.ds(i, 1), :],
                                      y[0:T, s, 105:107].rearrange("p (f j) -> p f j", f=1))
                c3.end()

            over(dve, NT, (0, divide), (1, low), (2, residual), (3, features))


GE_PARTS = ((0, 0, P), (1, P, GE - P))


def nibble_weights(sb):
    return dict(w1=sb("w1", [P, 2, GE]), w2n=sb("w2n", [P, 2, 2, GE]),
                w2=sb("w2", [P, 2, 2, GE]),
                w3=sb("w3", [P, 2, 2, 2]),
                b2=sb("b2", [P, 2, 2]),
                b3=sb("b3", [P, 2, 2]))


def load_nibble_weights(nc, sp, weights, w_in, Wa, ba, Ws, bs):
    w1, w2n, w3, b2, b3 = (weights[k] for k in ("w1", "w2n", "w3", "b2", "b3"))
    with nc.allow_non_contiguous_dma(reason="a few columns of small weights"):
        for q, (W, bias) in enumerate(((Wa, ba), (Ws, bs))):
            for r, f in ((0, 0), (1, 1), (2, 35), (3, 36)):
                sp.dma_start(w1[r:r + 1, q, :], W[0, :, f:f + 1].rearrange("o d -> d o")).then_inc(w_in, 16)
            sp.dma_start(w1[4:5, q, :], bias[0:1, :]).then_inc(w_in, 16)
            for n, o, m in GE_PARTS:
                sp.dma_start(w2n[0:m, q, n, :], W[1, o:o + m, :]).then_inc(w_in, 16)
                sp.dma_start(w3[0:m, q, n, :], W[2, 100:102, o:o + m].rearrange("o d -> d o")).then_inc(w_in, 16)
                sp.dma_start(b2[0:m, q, n:n + 1], bias[1:2, o:o + m].rearrange("o d -> d o")).then_inc(w_in, 16)
            sp.dma_start(b3[:, q, :], bias[2:3, 100:102].to_broadcast([P, 2])).then_inc(w_in, 16)
    return 2 * (5 + 6 + 1)


def nibble_pipelines(nc, sb_in, ident, weights, nib, opc, res):
    G = 2
    C = G * 2 * T
    NG = -(-NT // G)

    def tiles_of(g):
        return NT - (NG - 1) * G if isinstance(g, int) and g == NG - 1 else G

    with phase(nc) as sem, ExitStack() as ph:
        sb = sb_in(ph)
        set_ = sb("nib_set", [P, NT, 4])
        val = sb("nib_val", [P, NT, 4])
        feat = sb("feat", [P, NT + 1, 2, 5])
        w1, w2, w3, b2, b3 = (weights[k] for k in ("w1", "w2", "w3", "b2", "b3"))
        fst = sb("fst", [P, 2, G * 2, 5])
        fT = sb("fT", [P, 2, C])
        h1 = sb("h1", [P, 2, 2, 2, C])
        h2 = sb("h2", [P, 2, 2, 2, C])
        w1p = sb("w1p", [P, 2, GE])
        w3p = sb("w3p", [P, 2, 2, 4])
        r3T = sb("r3T", [4, NT * 2 * T])
        psF = ph.enter_context(nc.psum_tensor("psF", [P, 512], F32))
        ps1 = ph.enter_context(nc.psum_tensor("ps1", [P, 2, 2, 512], F32))
        ps2 = ph.enter_context(nc.psum_tensor("ps2", [P, 2, 512], F32))
        ps3 = ph.enter_context(nc.psum_tensor("ps3", [P, 512], F32))
        chain = sem("p5_chain")
        padded, staged, f_psum, f_ready, w3_ready, l1, r1, l2, r2, l3, r3, r_psum = (
            sem("p5_" + n) for n in ("padded", "staged", "f_psum", "f_ready", "w3_ready", "l1", "r1", "l2", "r2", "l3",
                                     "r3", "r_psum"))
        block = ph.enter_context(nc.Block())

        @block.gpsimd
        def _(pool):
            nc.gpsimd.memset(w1p[:], 0.0).then_inc(padded, 1)
            nc.gpsimd.memset(fT[:], 0.0).then_inc(padded, 1)
            pool.wait_ge(padded, 1)
            nc.gpsimd.tensor_copy(w1p[0:5], w1[0:5]).then_inc(padded, 1)
            nc.gpsimd.memset(h1[:, :, :, 1, :], 0.0).then_inc(padded, 1)
            nc.gpsimd.memset(h2[:, :, :, 1, :], 0.0).then_inc(padded, 1)

        @block.vector
        def _(dve):
            c = Chain(dve, chain)
            for first, end in ((GE - P, 64), (64, P)):
                nc.vector.memset(w2[first:end, :, 1, :], 0.0)
            c.link(nc.vector.memset(w3p[:], 0.0))
            for q in range(2):
                for n, o, m in GE_PARTS:
                    t = nc.vector.tensor_copy(w3p[0:m, q, n, 2 * q:2 * q + 2], w3[0:m, q, n, :])
            t.then_inc(w3_ready, 1)
            c.link(nc.vector.memset(feat[:], 1.0))
            c.link(nc.vector.tensor_scalar(set_[0:T], nib[0:T], 0.0, None, ALU.is_gt))
            c.link(nc.vector.tensor_scalar(val[0:T], nib[0:T], -1.0, 16.0, ALU.mult, ALU.add))
            c.link(nc.vector.tensor_tensor(val[0:T], val[0:T], set_[0:T], ALU.mult))
            for a in range(2):
                c.link(nc.vector.tensor_copy(feat[0:T, 0:NT, :, a], val[0:T, :, 2 * a:2 * a + 2]))
            for p in range(2):
                c.link(nc.vector.tensor_copy(feat[0:T, 0:NT, p, 2:4], opc[0:T]))
            def stage(g, s):
                dve.wait_ge(f_psum, g + 1)
                k = tiles_of(g)
                nc.vector.tensor_copy(fst[0:T, s, 0:k * 2, :].rearrange("p (t q) f -> p t (q f)", q=2),
                                      feat[0:T, bass.ds(g * G, k), :, :].rearrange("p t q f -> p t (q f)")
                                      ).then_inc(staged, 1)

            over(dve, NG, (0, stage), peel=1)
            dve.wait_ge(r_psum, 1)
            back = psF[0:T, 0:NT * 8].rearrange("p (t a q r) -> p t a q r", a=2, q=2, r=2)
            for q in range(2):
                for a in range(2):
                    nc.vector.tensor_tensor(res[0:T, :, q, a, :], back[:, :, a, q, :],
                                            b3[0:T, q, :].rearrange("p (o r) -> p o r", o=1).to_broadcast([T, NT, 2]),
                                            ALU.add)

        @block.scalar
        def _(act):
            def features(g, s):
                act.wait_ge(f_psum, g + 3)
                act.wait_ge(l1, 2 * g + 2)
                cols = tiles_of(g) * 2 * T
                nc.scalar.copy(fT[0:5, s, 0:cols], psF[0:5, 0:cols]).then_inc(f_ready, 1)

            def layer1(q):
                def rectify(g, s):
                    act.wait_ge(l1, 2 * g + q + 5)
                    cols = tiles_of(g) * 2 * T
                    for n, o, m in GE_PARTS:
                        t = nc.scalar.activation(h1[0:m, s, q, n, 0:cols], ps1[0:m, q, n, 0:cols], ACT.Relu)
                    t.then_inc(r1, 1)

                return rectify

            def layer2(q):
                def rectify(g, s):
                    act.wait_ge(l2, 2 * g + q + 1)
                    cols = tiles_of(g) * 2 * T
                    for n, o, m in GE_PARTS:
                        t = nc.scalar.activation(h2[0:m, s, q, n, 0:cols], ps2[0:m, n, 0:cols], ACT.Relu,
                                                 bias=b2[0:m, q, n:n + 1])
                    t.then_inc(r2, 1)

                return rectify

            def results(g, s):
                act.wait_ge(l3, g + 1)
                cols = tiles_of(g) * 2 * T
                nc.scalar.copy(r3T[:, bass.ds(g * C, cols)], ps3[0:4, 0:cols]).then_inc(r3, 1)

            act.wait_ge(padded, 5)
            over(act, NG, (0, features), (4, results), (1, layer1(0)), (2, layer2(0)), (1, layer1(1)),
                 (2, layer2(1)), peel=1)

        @block.tensor
        def _(pe):
            pe.sem_inc(f_psum, 2)
            pe.sem_inc(l1, 4)
            pe.sem_inc(f_ready, 1)
            pe.sem_inc(r1, 2)
            pe.sem_inc(r2, 1)
            pe.sem_inc(r3, 1)

            def features(g, s):
                pe.wait_ge(staged, g + 1)
                pe.wait_ge(f_ready, g + 1)
                for j in range(tiles_of(g) * 2):
                    t = nc.tensor.transpose(psF[0:5, j * T:(j + 1) * T], fst[0:T, s, j, :], ident[0:T, 0:T])
                t.then_inc(f_psum, 1)

            def layer1(q):
                def products(g, s):
                    pe.wait_ge(f_ready, g + 2)
                    pe.wait_ge(r1, 2 * g + q + 1)
                    cols = tiles_of(g) * 2 * T
                    for n, o, m in GE_PARTS:
                        t = nc.tensor.matmul(ps1[0:m, q, n, 0:cols], w1p[:, q, o:o + m], fT[:, s, 0:cols],
                                             start=True, stop=True)
                    t.then_inc(l1, 1)

                return products

            def layer2(q):
                def products(g, s):
                    cols = tiles_of(g) * 2 * T
                    pe.wait_ge(r1, 2 * g + q + 3)
                    pe.wait_ge(r2, 2 * g + q + 1)
                    for n, o, m in GE_PARTS:
                        for n1, o1, m1 in GE_PARTS:
                            t = nc.tensor.matmul(ps2[0:m, n, 0:cols], w2[:, q, n1, o:o + m],
                                                 h1[:, s, q, n1, 0:cols], start=(n1 == 0), stop=(n1 == 1))
                    t.then_inc(l2, 1)

                return products

            def layer3(g, s):
                cols = tiles_of(g) * 2 * T
                pe.wait_ge(r2, 2 * g + 3)
                pe.wait_ge(r3, g + 1)
                for q in range(2):
                    for n, o, m in GE_PARTS:
                        t = nc.tensor.matmul(ps3[0:4, 0:cols], w3p[:, q, n, :], h2[:, s, q, n, 0:cols],
                                             start=(q + n == 0), stop=(q + n == 2))
                t.then_inc(l3, 1)

            pe.wait_ge(w3_ready, 1)
            pe.wait_ge(padded, 5)
            over(pe, NG, (0, features), (1, layer1(0)), (2, layer2(0)), (1, layer1(1)), (2, layer2(1)), (3, layer3),
                 peel=1)
            pe.wait_ge(r3, NG + 1)
            for n in range(NT * 2):
                t = nc.tensor.transpose(psF[0:T, n * 4:(n + 1) * 4], r3T[:, n * T:(n + 1) * T], ident[0:4, 0:4])
            t.then_inc(r_psum, 1)


def alu_out(nc, sb_in, eps, marks, res, acc, dis, x2, g_d):
    with phase(nc) as sem, ExitStack() as ph:
        sb = sb_in(ph)
        madd = sb("madd", [P, NT])
        msub = sb("msub", [P, NT])
        not_add = sb("not_add", [P, NT])
        twice = sb("twice", [P, NT])
        pick = sb("pick", [P, NT, 4])
        tmp = sb("tmp", [P, NT, 4])
        iota16_i = sb("iota16_i", [P, 16], I32)
        iota16 = sb("iota16", [P, 16])
        hot = sb("hot", [P, NT, 2, 16])
        carry = sb("carry", [P, NT])
        stats = sb("stats6", [P, 2, 6])
        mv = sb("mv6", [P, 2, 2])
        std = sb("std6", [P, 2, 1])
        rstd = sb("rstd6", [P, 2, 1])
        i_ready, chain, chain2, chain3, carrier, var_ready, std_ready, g_ready, g_out = (
            sem("p6_" + n) for n in ("iota_ready", "chain", "chain2", "chain3", "carrier", "var_ready", "std_ready",
                                     "g_ready", "g_out"))
        block = ph.enter_context(nc.Block())

        @block.gpsimd
        def _(pool):
            nc.gpsimd.iota(iota16_i[:], [[1, 16]], base=0, channel_multiplier=0).then_inc(i_ready, 1)

        @block.sync
        def _(sp):
            def store(i, s):
                sp.wait_ge(g_ready, i + 1)
                sp.dma_start(g_d[rows(i), :], acc[0:T, bass.ds(i * AW, D)]).then_inc(g_out, 16)

            over(sp, NT, (0, store))
            sp.wait_ge(g_out, 16 * NT)

        @block.scalar
        def _(act):
            def root(i, s):
                act.wait_ge(var_ready, i + 1)
                nc.scalar.activation(std[0:T, s, :], mv[0:T, s, 1:2], ACT.Sqrt, bias=eps[0:T, :]).then_inc(std_ready, 1)

            over(act, NT, (0, root))

        @block.vector
        def _(dve):
            c = Chain(dve, chain)
            v = nc.vector
            m0, m1, m2 = (marks[0:T, :, j] for j in range(3))
            c.link(v.tensor_tensor(madd[0:T], m0, m1, ALU.mult))
            c.link(v.tensor_scalar(not_add[0:T], m1, -1.0, 1.0, ALU.mult, ALU.add))
            c.link(v.tensor_tensor(msub[0:T], m0, m2, ALU.mult))
            c.link(v.tensor_tensor(msub[0:T], msub[0:T], not_add[0:T], ALU.mult))
            for m, q, to in ((madd, 0, pick), (msub, 1, tmp)):
                c.link(v.tensor_tensor(to[0:T], res[0:T, :, q].rearrange("p t a b -> p t (a b)"),
                                       m[0:T].rearrange("p (t o) -> p t o", o=1).to_broadcast([T, NT, 4]), ALU.mult))
            c.link(v.tensor_tensor(pick[0:T], pick[0:T], tmp[0:T], ALU.add))
            c.link(v.tensor_tensor(twice[0:T], madd[0:T], msub[0:T], ALU.add))
            c.link(v.tensor_scalar(carry[0:T], pick[0:T, :, 3], 0.5, None, ALU.is_gt))
            c.link(v.tensor_tensor(carry[0:T], carry[0:T], twice[0:T], ALU.mult))
            c.link(v.tensor_scalar(twice[0:T], twice[0:T], 2.0, None, ALU.mult))
            c.link(v.tensor_scalar(pick[0:T], pick[0:T], 0.0, 15.0, ALU.max, ALU.min))
            c.link(v.tensor_scalar(pick[0:T], pick[0:T], RNE, None, ALU.add))
            c.link(v.tensor_scalar(pick[0:T], pick[0:T], -RNE, None, ALU.add))
            dve.wait_ge(i_ready, 1)
            c.link(v.tensor_copy(iota16[:], iota16_i[:]))
            for p in range(2):
                c.link(v.tensor_tensor(hot[0:T, :, p, :],
                                       iota16[0:T, :].rearrange("p (o j) -> p o j", o=1).to_broadcast([T, NT, 16]),
                                       pick[0:T, :, 2 * p:2 * p + 1].to_broadcast([T, NT, 16]), ALU.is_equal))
            c.link(v.tensor_tensor(hot[0:T].rearrange("p t a j -> p t (a j)"),
                                   hot[0:T].rearrange("p t a j -> p t (a j)"),
                                   twice[0:T].rearrange("p (t o) -> p t o", o=1).to_broadcast([T, NT, 32]), ALU.mult))
            x2t = x2[0:T, :].rearrange("p (t d) -> p t d", t=NT)
            c.link(v.tensor_tensor(x2t[:, :, 128:160], x2t[:, :, 128:160],
                                   hot[0:T].rearrange("p t a j -> p t (a j)"), ALU.add))
            c.link(v.tensor_tensor(x2t[:, :, 160], x2t[:, :, 160], carry[0:T], ALU.add))
            c2, c3 = Chain(dve, chain2, 1), Chain(dve, chain3, 2)

            def statistics(i, s):
                c2.start(i)
                c2.link(v.bn_stats(stats[0:T, s, :], x2[0:T, bass.ds(i * D, D)]))
                dve.sem_inc(carrier, 1)
                v.bn_aggr(mv[0:T, s, :], stats[0:T, s, :]).then_inc(var_ready, 1)
                c2.end()

            def normalize(i, s):
                c3.start(i)
                dve.wait_ge(std_ready, i + 1)
                c3.link(v.reciprocal(rstd[0:T, s, :], std[0:T, s, :]))
                c3.link(v.tensor_tensor(rstd[0:T, s, :], rstd[0:T, s, :], dis[0:T, bass.ds(i, 1)], ALU.mult))
                v.tensor_scalar(acc[0:T, bass.ds(i * AW, D)], x2[0:T, bass.ds(i * D, D)], mv[0:T, s, 0:1],
                                rstd[0:T, s, 0:1], ALU.subtract, ALU.mult).then_inc(g_ready, 1)
                c3.end()

            over(dve, NT, (0, statistics), (1, normalize))


def product3(nc, out, a, b, start, stop):
    nc.tensor.matmul(out, a[0], b[1], start=start, stop=False)
    nc.tensor.matmul(out, a[1], b[0], start=False, stop=False)
    return nc.tensor.matmul(out, a[0], b[0], start=False, stop=stop)


def gcn_dense(nc, sb_in, n, ident, W, b, acc, dis, x2, g_d):
    last = n == 2
    with phase(nc) as sem, ExitStack() as ph:
        sb = sb_in(ph)
        w = sb(f"w_gcn{n}", [P, KT, D])
        w_hi = sb(f"w_hi{n}", [P, KT, D], F32R)
        w_lo = sb(f"w_lo{n}", [P, KT, D], F32R)
        bias = sb(f"b_gcn{n}", [P, D])
        z = sb(f"z{n}", [P, 2, D])
        z_hi = sb(f"z_hi{n}", [P, 2, KT * T], F32R)
        z_lo = sb(f"z_lo{n}", [P, 2, KT * T], F32R)
        h = sb(f"h_gcn{n}", [P, 2, D])
        psT = ph.enter_context(nc.psum_tensor(f"psTg{n}", [P, 2, 512], F32))
        psM = ph.enter_context(nc.psum_tensor(f"psMg{n}", [P, 2, 512], F32))
        w_in, whi_ready, wlo_ready, z_ready, zT_psum, hi_ready, lo_ready, m_ready, h_ready, g_ready = (
            sem(f"g{n}_{k}") for k in ("w_in", "whi_ready", "wlo_ready", "z_ready", "zT_psum", "hi_ready", "lo_ready",
                                       "m_ready", "h_ready", "g_ready"))
        g_out, carrier = [sem(f"g{n}_out0"), sem(f"g{n}_out1")], sem(f"g{n}_carrier")
        block = ph.enter_context(nc.Block())

        @block.sync
        def _(sp):
            sp.dma_start(w[:], W.rearrange("(k p) n -> p k n", p=P)).then_inc(w_in, 16)
            sp.dma_start(bias[:], b.rearrange("(o n) -> o n", o=1).to_broadcast([P, D])).then_inc(w_in, 16)

            def store(i, s):
                if last:
                    sp.wait_ge(g_ready, i + 1)
                    sp.dma_start(g_d[rows(i), :], h[0:T, s, :]).then_inc(g_out[s], 16)
                else:
                    sp.wait_ge(g_ready, i + 3)
                    sp.dma_start(g_d[rows(i), :], acc[0:T, bass.ds(i * AW, D)]).then_inc(g_out[s], 16)

            over(sp, NT, (0, store))
            granted = 16 if last else 0
            sp.wait_ge(g_out[0], 16 * (NT // 2 + 1) + granted)
            sp.wait_ge(g_out[1], 16 * (NT // 2) + granted)

        @block.gpsimd
        def _(pool):
            def take(i, s):
                pool.wait_ge(zT_psum, i + 1)
                pool.sem_inc(carrier, 1)
                nc.gpsimd.tensor_copy(z[0:T, s, :], acc[0:T, bass.ds(i * AW, D)]).then_inc(z_ready, 1)

            over(pool, NT, (0, take))

        @block.tensor
        def _(pe):
            pe.sem_inc(zT_psum, 2)
            pe.sem_inc(m_ready, 2)

            def transposes(i, s):
                pe.wait_ge(z_ready, i + 1)
                pe.wait_ge(lo_ready, i + 1)
                for k in range(KT):
                    t = nc.tensor.transpose(psT[:, s, k * T:(k + 1) * T], z[0:T, s, k * P:(k + 1) * P],
                                            ident[0:T, 0:T])
                t.then_inc(zT_psum, 1)

            def product(i, s):
                if isinstance(i, int) and i == 0:
                    pe.wait_ge(wlo_ready, 1)
                pe.wait_ge(lo_ready, i + 3)
                pe.wait_ge(h_ready, i + 1)
                for k in range(KT):
                    c = slice(k * T, (k + 1) * T)
                    t = product3(nc, psM[0:T, s, :], (z_hi[:, s, c], z_lo[:, s, c]), (w_hi[:, k, :], w_lo[:, k, :]),
                                 k == 0, k == KT - 1)
                t.then_inc(m_ready, 1)

            over(pe, NT, (0, transposes), (1, product))

        @block.scalar
        def _(act):
            if not last:
                act.sem_inc(g_ready, 2)
            act.wait_ge(w_in, 32)
            nc.scalar.copy(w_hi[:], w[:]).then_inc(whi_ready, 1)

            def high(i, s):
                act.wait_ge(zT_psum, i + 3)
                act.wait_ge(m_ready, i + 1)
                nc.scalar.copy(z_hi[:, s, :], psT[:, s, 0:KT * T]).then_inc(hi_ready, 1)

            def rectify(i, s):
                if not last:
                    act.wait_ge(h_ready, i + 3)
                    nc.scalar.activation(acc[0:T, bass.ds(i * AW, D)], h[0:T, s, :], ACT.Relu,
                                         scale=dis[0:T, bass.ds(i, 1)]).then_inc(g_ready, 1)

            over(act, NT, (0, high), (2, rectify))

        @block.vector
        def _(dve):
            dve.sem_inc(h_ready, 2)
            dve.sem_inc(lo_ready, 2)
            if last:
                dve.sem_inc(g_out[0], 16)
                dve.sem_inc(g_out[1], 16)
            dve.wait_ge(whi_ready, 1)
            nc.vector.tensor_tensor(w_lo[:], w[:], w_hi[:].bitcast(F32), ALU.subtract).then_inc(wlo_ready, 1)

            def low(i, s):
                dve.wait_ge(hi_ready, i + 1)
                nc.vector.tensor_tensor(z_lo[:, s, :], psT[:, s, 0:KT * T], z_hi[:, s, :].bitcast(F32),
                                        ALU.subtract).then_inc(lo_ready, 1)

            def add_bias(i, s):
                dve.wait_ge(m_ready, i + 3)
                if last:
                    dve.wait_ge(g_out[s], lap(i, s))
                else:
                    dve.wait_ge(g_ready, i + 1)
                nc.vector.scalar_tensor_tensor(out=h[0:T, s, :], in0=psM[0:T, s, :], scalar=dis[0:T, bass.ds(i, 1)],
                                               in1=bias[0:T, :], op0=ALU.mult, op1=ALU.add).then_inc(h_ready, 1)
                if last:
                    dve.wait_ge(h_ready, i + 3)
                    nc.vector.tensor_tensor(h[0:T, s, :], h[0:T, s, :], x2[0:T, bass.ds(i * D, D)],
                                            ALU.add).then_inc(g_ready, 1)

            over(dve, NT, (0, low), (1, add_bias))


class Ternary:

    PG = 4

    def __init__(self, nc, sem, sb, ph, ident, w_gate, w_up, w_down, wT_d):
        self.nc, self.ident = nc, ident
        self.runs = [(w_gate, wT_d[0], 0, KT, FT), (w_up, wT_d[1], 0, KT, FT)]
        self.runs += [(w_down, wT_d[2], g, min(self.PG, FT - g), KT) for g in range(0, FT, self.PG)]
        self.pieces = sum(r[4] for r in self.runs)
        wide = self.PG * P
        self.w, self.wT = sb("t_w", [P, 2, wide]), sb("t_wT", [P, 2, wide])
        self.up, self.down = sb("t_up", [P, wide]), sb("t_down", [P, wide])
        self.total, self.scale, self.half, self.nhalf = (sb(f"t_{k}", [P, self.PG]) for k in
                                                         ("total", "scale", "half", "nhalf"))
        self.ps = ph.enter_context(nc.psum_tensor("t_ps", [P, 2, 512], F32))
        self.chain, self.quantized, self.turned, self.placed, self.carrier, self.blank = (
            sem("t_" + k) for k in ("chain", "quantized", "turned", "placed", "carrier", "blank"))
        self.w_in, self.w_out = [sem("t_in0"), sem("t_in1")], [sem("t_out0"), sem("t_out1")]

    def each(self, eng, *stages):
        first = 0
        for run in self.runs:
            over(eng, run[4], *((lag, lambda m, s, f=f, k=first, run=run: f(m + k, (s + k) % 2, run, m))
                                for lag, f in stages))
            first += run[4]

    def loads_and_stores(self, sp):
        sp.sem_inc(self.turned, 2)

        def load(n, s, run, m):
            src, _, g0, groups, _ = run
            sp.wait_ge(self.turned, n + 1)
            sp.sem_inc(self.carrier, 1)
            sp.dma_start(self.w[:, s, 0:groups * P],
                         src[bass.ds(m * P, P), g0 * P:(g0 + groups) * P]).then_inc(self.w_in[s], 16)

        def store(n, s, run, m):
            _, dst, g0, groups, _ = run
            sp.wait_ge(self.placed, n + 3)
            sp.sem_inc(self.carrier, 1)
            sp.dma_start(dst[:, g0:g0 + groups, bass.ds(m * P, P)],
                         self.wT[:, s, 0:groups * P].rearrange("p (g k) -> p g k", g=groups)
                         ).then_inc(self.w_out[s], 16)

        self.each(sp, (0, load), (1, store))
        sp.wait_ge(self.w_out[0], 16 * ((self.pieces + 1) // 2 + 1))
        sp.wait_ge(self.w_out[1], 16 * (self.pieces // 2 + 1))

    def quantize(self, dve):
        v = self.nc.vector
        c = Chain(dve, self.chain, 7)

        def piece(n, s, run, m):
            groups = run[3]
            c.start(n)
            dve.wait_ge(self.w_in[s], lap(n, s))
            wt, ut, dt = self.w[:, s, 0:groups * P], self.up[:, 0:groups * P], self.down[:, 0:groups * P]
            c.link(v.tensor_reduce(self.total[:, 0:groups], wt.rearrange("p (g k) -> p g k", g=groups), AX.X,
                                   ALU.add, apply_absolute_value=True))
            c.link(v.tensor_scalar(self.scale[:], self.total[:], 1.0 / P, EPS, ALU.mult, ALU.add))
            v.tensor_scalar(self.half[:], self.scale[:], 0.5, None, ALU.mult)
            c.link(v.tensor_scalar(self.nhalf[:], self.scale[:], -0.5, None, ALU.mult))
            for g in range(groups):
                k = slice(g * P, (g + 1) * P)
                v.tensor_scalar(self.up[:, k], self.w[:, s, k], self.half[:, g:g + 1], self.scale[:, g:g + 1],
                                ALU.is_gt, ALU.mult)
                t = v.tensor_scalar(self.down[:, k], self.w[:, s, k], self.nhalf[:, g:g + 1],
                                    self.scale[:, g:g + 1], ALU.is_lt, ALU.mult)
            c.link(t)
            c.link(v.tensor_tensor(ut, ut, dt, ALU.subtract))
            c.link(v.tensor_tensor(ut, ut, wt, ALU.subtract))
            c.link(v.tensor_tensor(wt, wt, ut, ALU.add))
            dve.sem_inc(self.quantized, 1)
            c.end()

        v.memset(self.total[:], 0.0).then_inc(self.blank, 1)
        dve.wait_ge(self.blank, 1)
        self.each(dve, (0, piece))

    def transpose(self, pe):
        def piece(n, s, run, m):
            pe.wait_ge(self.quantized, n + 1)
            pe.wait_ge(self.placed, n + 1)
            for g in range(run[3]):
                t = self.nc.tensor.transpose(self.ps[:, s, g * P:(g + 1) * P], self.w[:, s, g * P:(g + 1) * P],
                                             self.ident[:])
            t.then_inc(self.turned, 1)

        self.each(pe, (0, piece))

    def place(self, act):
        act.sem_inc(self.placed, 2)
        act.sem_inc(self.w_out[0], 16)
        act.sem_inc(self.w_out[1], 16)

        def piece(n, s, run, m):
            act.wait_ge(self.turned, n + 3)
            act.wait_ge(self.w_out[s], lap(n, s))
            wide = run[3] * P
            self.nc.scalar.copy(self.wT[:, s, 0:wide], self.ps[:, s, 0:wide]).then_inc(self.placed, 1)

        self.each(act, (0, piece))


def swiglu(nc, sb_in, ident, eps, wT_d, x3_d, out):
    G = 3
    C = G * T + G * T % 2
    NG = NT // G
    RAW, QF = 4, FF // 2
    EARLY_F = 4
    with phase(nc) as sem, ExitStack() as ph:
        sb = sb_in(ph)
        wT = [[sb(f"w{k}T_{part}", shape, F32R) for part in ("hi", "lo")]
              for k, shape in (("g", [P, KT, FF]), ("u", [P, KT, FF]), ("d", [P, FT, D]))]
        xt = sb("xt8", [P, G, D])
        xr = sb("xr8", [P, G, D])
        stats = sb("stats8", [P, G, 6])
        mv = sb("mv8", [P, G, 2])
        std = sb("std8", [P, G])
        yT = [sb("yT_hi", [P, KT, C], F32R), sb("yT_lo", [P, KT, C], F32R)]
        sg = sb("sg", [P, 2, C])
        hid = sb("hid", [P, 2, C])
        hT = [sb("hT_hi", [P, FT, C], F32R), sb("hT_lo", [P, FT, C], F32R)]
        raw = sb("w_raw", [P, RAW, QF])
        psT = ph.enter_context(nc.psum_tensor("psT8", [P, 512], F32))
        psG = ph.enter_context(nc.psum_tensor("psG", [P, 2, 512], F32))
        psU = ph.enter_context(nc.psum_tensor("psU", [P, 2, 512], F32))
        psD = ph.enter_context(nc.psum_tensor("psD", [P, G, 512], F32))
        x_in, r_in, o_out = ([sem(f"f_{k}{j}") for j in range(G)] for k in ("x_in", "r_in", "o_out"))
        w_in = [sem(f"f_w_in{r}") for r in range(RAW)]
        (chain1, chain2, carrier, cleared, whi, wlo, var_ready, std_ready, yT_psum, yhi, ylo, gu, sig, prod, hhi, hlo,
         d_ready, o_ready) = (sem("f_" + k) for k in (
             "chain1", "chain2", "carrier", "cleared", "whi", "wlo", "var_ready", "std_ready", "yT_psum", "yhi", "ylo",
             "gu", "sig", "prod", "hhi", "hlo", "d_ready", "o_ready"))

        pieces = [(w, q) for w in range(3) for q in range(KT * FF // QF)]
        early = len(pieces) // 3 * 2

        def part(t, q):
            return t[:].rearrange("p a b -> p (a b)")[:, q * QF:(q + 1) * QF]

        block = ph.enter_context(nc.Block())

        def over_groups(eng, group):
            cols = T + T % 2
            group(0, G, C, G)
            with eng.Fori(1, NG - 1) as g:
                group(g, G, C, G)
            group(NG - 1, G, C, NT - NG * G)
            group(NG, NT - NG * G, cols, 0)

        @block.sync
        def _(sp):
            def load_weights(some):
                for n in some:
                    w, q = pieces[n]
                    if n >= RAW:
                        sp.wait_ge(wlo, n - RAW + 1)
                    sp.dma_start(raw[:, n % RAW, :], part(wT_d[w], q)).then_inc(w_in[n % RAW], 16)

            def load(g, tiles):
                for j in range(tiles):
                    sp.wait_ge(yT_psum, g * G + j + 1)
                    sp.dma_start(xt[0:T, j, :], x3_d[rows(g * G + j), :]).then_inc(x_in[j], 16)

            def group(g, tiles, cols, following):
                load(g + 1, following)
                if isinstance(g, int) and g == 0:
                    load_weights(range(early, len(pieces)))
                for j in range(tiles):
                    sp.wait_ge(o_out[j], 16 * g + 16)
                    sp.dma_start(xr[0:T, j, :], x3_d[rows(g * G + j), :]).then_inc(r_in[j], 16)
                for j in range(tiles):
                    sp.wait_ge(o_ready, g * G + j + G + 1)
                    sp.dma_start(out[rows(g * G + j), :], xr[0:T, j, :]).then_inc(o_out[j], 16)

            for j in range(G):
                sp.sem_inc(o_out[j], 16)
            load(0, G)
            load_weights(range(early))
            over_groups(sp, group)
            for j in range(G):
                sp.wait_ge(o_out[j], 16 * (NG + (2 if j < NT - NG * G else 1)))

        @block.vector
        def _(dve):
            c1, c2 = Chain(dve, chain1, 1), Chain(dve, chain2, 2)

            def split_weights(n):
                w, q = pieces[n]
                dve.wait_ge(whi, n + 1)
                nc.vector.tensor_tensor(part(wT[w][1], q), raw[:, n % RAW, :], part(wT[w][0], q).bitcast(F32),
                                        ALU.subtract).then_inc(wlo, 1)

            def statistics(g, tiles):
                for j in range(tiles):
                    c1.start(g * G + j)
                    dve.wait_ge(x_in[j], 16 * g + 16)
                    c1.link(nc.vector.bn_stats(stats[0:T, j, :], xt[0:T, j, :]))
                    dve.sem_inc(carrier, 1)
                    nc.vector.bn_aggr(mv[0:T, j, :], stats[0:T, j, :]).then_inc(var_ready, 1)
                    c1.end()

            def normalize(g, tiles):
                for j in range(tiles):
                    c2.start(g * G + j)
                    dve.wait_ge(std_ready, g * G + j + 1)
                    c2.link(nc.vector.reciprocal(std[0:T, j:j + 1], std[0:T, j:j + 1]))
                    c2.link(nc.vector.tensor_scalar(xt[0:T, j, :], xt[0:T, j, :], mv[0:T, j, 0:1],
                                                    std[0:T, j:j + 1], ALU.subtract, ALU.mult))
                    c2.end()

            def low_y(g, j):
                dve.wait_ge(yhi, g * G + j + 1)
                nc.vector.tensor_tensor(
                    yT[1][:, :, j * T:(j + 1) * T], psT[:, 0:KT * T].rearrange("p (k t) -> p k t", k=KT),
                    yT[0][:, :, j * T:(j + 1) * T].bitcast(F32), ALU.subtract).then_inc(ylo, 1)

            def group(g, tiles, cols, following):
                def low(f):
                    n, s = g * FT + f, f % 2
                    dve.wait_ge(hhi, n + 1)
                    nc.vector.tensor_tensor(hT[1][:, f, 0:cols], hid[:, s, 0:cols],
                                            hT[0][:, f, 0:cols].bitcast(F32), ALU.subtract).then_inc(hlo, 1)

                for f in range(FT):
                    n, s = g * FT + f, f % 2
                    dve.wait_ge(sig, n + 1)
                    dve.wait_ge(hlo, n + 1)
                    nc.vector.tensor_tensor(hid[:, s, 0:cols], sg[:, s, 0:cols], psU[:, s, 0:cols],
                                            ALU.mult).then_inc(prod, 1)
                    if f:
                        low(f - 1)
                    if isinstance(g, int) and g == 0 and early + f < len(pieces):
                        split_weights(early + f)
                    if f == EARLY_F:
                        statistics(g + 1, following)
                    if f == EARLY_F + 2:
                        normalize(g + 1, following)
                low(FT - 1)
                for j in range(G):
                    if j < following:
                        low_y(g + 1, j)
                    if j < tiles:
                        dve.wait_ge(d_ready, g * G + j + 1)
                        dve.wait_ge(r_in[j], 16 * g + 16)
                        nc.vector.tensor_tensor(xr[0:T, j, :], psD[0:T, j, :], xr[0:T, j, :],
                                                ALU.add).then_inc(o_ready, 1)

            dve.sem_inc(o_ready, G)
            dve.sem_inc(prod, 2)
            dve.sem_inc(hlo, 2)
            for yp in yT:
                nc.vector.memset(yp[:].bitcast(F32), 0.0).then_inc(cleared, 1)
            statistics(0, G)
            normalize(0, G)
            dve.wait_ge(cleared, 2)
            for j in range(G):
                low_y(0, j)
            for n in range(early):
                split_weights(n)
            over_groups(dve, group)

        @block.scalar
        def _(act):
            def split_weights(n):
                w, q = pieces[n]
                act.wait_ge(w_in[n % RAW], 16 * (n // RAW + 1))
                nc.scalar.copy(part(wT[w][0], q), raw[:, n % RAW, :]).then_inc(whi, 1)

            def roots(g, tiles):
                for j in range(tiles):
                    act.wait_ge(var_ready, g * G + j + 1)
                    nc.scalar.activation(std[0:T, j:j + 1], mv[0:T, j, 1:2], ACT.Sqrt,
                                         bias=eps[0:T, :]).then_inc(std_ready, 1)

            def high_y(g, tiles):
                for j in range(tiles):
                    act.wait_ge(yT_psum, g * G + j + G + 1)
                    nc.scalar.copy(yT[0][:, :, j * T:(j + 1) * T],
                                   psT[:, 0:KT * T].rearrange("p (k t) -> p k t", k=KT)).then_inc(yhi, 1)

            def group(g, tiles, cols, following):
                def high(f):
                    act.wait_ge(prod, g * FT + f + 3)
                    nc.scalar.copy(hT[0][:, f, 0:cols], hid[:, f % 2, 0:cols]).then_inc(hhi, 1)

                for f in range(FT):
                    n, s = g * FT + f, f % 2
                    act.wait_ge(gu, n + 1)
                    act.wait_ge(prod, n + 1)
                    nc.scalar.activation(sg[:, s, 0:cols], psG[:, s, 0:cols], ACT.Silu).then_inc(sig, 1)
                    if f:
                        high(f - 1)
                    if isinstance(g, int) and g == 0 and early + f < len(pieces):
                        split_weights(early + f)
                    if f == EARLY_F + 1:
                        roots(g + 1, following)
                high(FT - 1)
                high_y(g + 1, following)

            roots(0, G)
            act.wait_ge(cleared, 2)
            high_y(0, G)
            for n in range(early):
                split_weights(n)
            over_groups(act, group)

        @block.tensor
        def _(pe):
            pe.sem_inc(yT_psum, G)

            def transposes(g, j):
                i = g * G + j
                pe.wait_ge(chain2, 2 * i + 2)
                if not isinstance(i, int) or i:
                    pe.wait_ge(ylo, i)
                for k in range(KT):
                    t = nc.tensor.transpose(psT[:, k * T:(k + 1) * T], xt[0:T, j, k * P:(k + 1) * P],
                                            ident[0:T, 0:T])
                t.then_inc(yT_psum, 1)

            def group(g, tiles, cols, following):
                pe.wait_ge(ylo, g * G + tiles)
                for f in range(FT):
                    n, s = g * FT + f, f % 2
                    pe.wait_ge(prod, n + 1)
                    for ps, w in ((psG, wT[0]), (psU, wT[1])):
                        for k in range(KT):
                            t = product3(nc, ps[:, s, 0:cols], [p[:, k, f * P:(f + 1) * P] for p in w],
                                         [p[:, k, 0:cols] for p in yT], k == 0, k == KT - 1)
                    t.then_inc(gu, 1)
                if isinstance(g, int) and g == 0:
                    pe.wait_ge(wlo, len(pieces))
                for j in range(G):
                    if j < following:
                        transposes(g + 1, j)
                    if j == 0:
                        pe.wait_ge(hlo, g * FT + FT + 2)
                    if j < tiles:
                        pe.wait_ge(o_ready, g * G + j + 1)
                        for f in range(FT):
                            t = product3(nc, psD[0:T, j, :], [p[:, f, j * T:(j + 1) * T] for p in hT],
                                         [p[:, f, :] for p in wT[2]], f == 0, f == FT - 1)
                        t.then_inc(d_ready, 1)

            for j in range(G):
                transposes(0, j)
            pe.wait_ge(wlo, early)
            over_groups(pe, group)


_INS = ['x', 'src', 'dst', 'L0_gnn_Wk', 'L0_gnn_bk', 'L0_gnn_Wq', 'L0_gnn_bq', 'L0_gnn_Wv', 'L0_gnn_bv',
        'L0_gnn_Wff', 'L0_gnn_bff', 'L0_ffn_Wa', 'L0_ffn_ba', 'L0_ffn_Ws', 'L0_ffn_bs', 'L1_gnn_W1', 'L1_gnn_b1',
        'L1_gnn_W2', 'L1_gnn_b2', 'L1_gnn_W3', 'L1_gnn_b3', 'L1_ffn_w_gate', 'L1_ffn_w_up', 'L1_ffn_w_down']


def kernel(**inputs):
    import concourse.bacc as bacc
    from concourse.bass_utils import run_bass_kernel_spmd

    nc = bacc.Bacc("TRN2", target_bir_lowering=False, num_devices=1)
    arrays, args = {}, []
    for name in _INS:
        a = np.ascontiguousarray(inputs[name])
        arrays[f"in_{name}"] = a
        args.append(nc.dram_tensor(f"in_{name}", a.shape, mybir.dt.from_np(a.dtype), kind="ExternalInput").ap())
    out = nc.dram_tensor("out", (N, D), F32, kind="ExternalOutput").ap()
    build(nc, *args, out)
    r = run_bass_kernel_spmd(nc, [arrays], core_ids=[0])
    return r.results[0]["out"]
```
